# Optimizing a Trainium2 kernel written in Bass

```python
import numpy as np
import jax
import jax.numpy as jnp

def _softmax(x, axis=-1):
    return jax.nn.softmax(x, axis=axis)

def _gelu(x):
    return jax.nn.gelu(x, approximate=True)

def _silu(x):
    return jax.nn.silu(x)

def _sigmoid(x):
    return jax.nn.sigmoid(x)

def _layernorm(x, axis=-1, eps=1e-05):
    m = jnp.mean(x, axis=axis, keepdims=True)
    v = jnp.var(x, axis=axis, keepdims=True)
    return (x - m) / jnp.sqrt(v + eps)

def _scatter_add(tgt, idx, src, axis=0):
    return tgt.at[idx].add(src)

def _segment_sum(src, seg, n):
    return jax.ops.segment_sum(src, seg, n)
kernel_name = 'mk_seq_preln_d1_jaxref_r8_38cda3'

def setup_inputs(seed: int=0):
    np.random.seed(seed)
    _w = jnp.asarray

    def _L0_attn_setup():
        import jax, jax.numpy as jnp
        import numpy as np
        HEADS, D_MODEL, D_V = (16, 128, 64)
        D_K = D_MODEL // HEADS
        key = jax.random.key(seed)
        k1, k2, k3, k4, k5 = jax.random.split(key, 5)
        B, T = (2, 256)
        s = 1.0 / np.sqrt(D_MODEL)
        return {'x': jax.random.normal(k1, (B, T, D_MODEL), dtype=jnp.float32), 'Wq': jax.random.normal(k2, (D_MODEL, HEADS * D_K), dtype=jnp.float32) * s, 'Wk': jax.random.normal(k3, (D_MODEL, HEADS * D_K), dtype=jnp.float32) * s, 'Wv': jax.random.normal(k4, (D_MODEL, HEADS * D_V), dtype=jnp.float32) * s, 'Wo': jax.random.normal(k5, (HEADS * D_V, D_MODEL), dtype=jnp.float32) * (1.0 / np.sqrt(HEADS * D_V))}
    _L0_attn_in = _L0_attn_setup()

    def _L0_ffn_setup():
        import jax, jax.numpy as jnp
        import numpy as np
        NUM_EXPERTS = 8
        EXPERT_CAPACITY = 2.0
        key = jax.random.key(seed)
        k1, k2, k3, k4 = jax.random.split(key, 4)
        B, T, C, H, E = (4, 512, 128, 512, NUM_EXPERTS)
        x = jax.random.normal(k1, (B, T, C), jnp.float32)
        gate_w = jax.random.normal(k2, (C, E), jnp.float32) * 0.02
        w1 = jax.random.normal(k3, (E, C, H), jnp.float32) * 0.02
        w2 = jax.random.normal(k4, (E, H, C), jnp.float32) * 0.02
        return {'x': x, 'gate_w': gate_w, 'w1': w1, 'w2': w2}
    _L0_ffn_in = _L0_ffn_setup()
    _d = {'L0_attn_x': _L0_attn_in['x'], 'L0_attn_Wq': _L0_attn_in['Wq'], 'L0_attn_Wk': _L0_attn_in['Wk'], 'L0_attn_Wv': _L0_attn_in['Wv'], 'L0_attn_Wo': _L0_attn_in['Wo'], 'L0_ffn_gate_w': _L0_ffn_in['gate_w'], 'L0_ffn_w1': _L0_ffn_in['w1'], 'L0_ffn_w2': _L0_ffn_in['w2']}
    _x0 = _d['L0_attn_x']
    _d['L0_attn_x'] = jax.random.normal(jax.random.fold_in(jax.random.key(seed), 1), (16, 256, 128), dtype=_x0.dtype)
    del _x0
    return _d

def reference(L0_attn_x, L0_attn_Wq, L0_attn_Wk, L0_attn_Wv, L0_attn_Wo, L0_ffn_gate_w, L0_ffn_w1, L0_ffn_w2):

    def _L0_attn_ref(x, Wq, Wk, Wv, Wo):
        import jax, jax.numpy as jnp
        import numpy as np
        HEADS, D_MODEL, D_V = (16, 128, 64)
        D_K = D_MODEL // HEADS
        B, T, _ = x.shape
        scale = jnp.asarray(np.sqrt(D_K), x.dtype)
        q = (x @ Wq).reshape(B, T, HEADS, D_K).transpose(0, 2, 1, 3)
        k = (x @ Wk).reshape(B, T, HEADS, D_K).transpose(0, 2, 1, 3)
        v = (x @ Wv).reshape(B, T, HEADS, D_V).transpose(0, 2, 1, 3)
        scores = jnp.einsum('bhqd,bhkd->bhqk', q, k) / scale
        causal = jnp.triu(jnp.ones((T, T), dtype=bool), k=1)
        scores = jnp.where(causal, jnp.asarray(-jnp.inf, scores.dtype), scores)
        attn = jax.nn.softmax(scores, axis=-1)
        ctx = jnp.einsum('bhqk,bhkd->bhqd', attn, v)
        out = ctx.transpose(0, 2, 1, 3).reshape(B, T, HEADS * D_V)
        return out @ Wo

    def _L0_ffn_ref(x, gate_w, w1, w2):
        import jax, jax.numpy as jnp
        import numpy as np
        NUM_EXPERTS = 8
        EXPERT_CAPACITY = 2.0
        B, T, C = x.shape
        E = gate_w.shape[1]
        cap = int(EXPERT_CAPACITY * T / E)
        scores = jnp.einsum('BTC,CE->BTE', x, gate_w)
        probs = jax.nn.softmax(scores, axis=-1)
        probs_et = jnp.transpose(probs, (0, 2, 1))
        top_p, top_idx = jax.lax.top_k(probs_et, cap)
        xin = jnp.take_along_axis(x[:, None, :, :], top_idx[..., None], axis=2)
        h = jax.nn.gelu(jnp.einsum('BElC,ECH->BElH', xin, w1), approximate=False)
        y = jnp.einsum('BElH,EHC->BElC', h, w2)
        y = y * top_p[..., None]
        b_idx = jnp.arange(B)[:, None, None]
        out = jnp.zeros((B, T, C), x.dtype).at[b_idx, top_idx].add(y)
        return out
    x = L0_attn_x
    x = x + _L0_attn_ref(_layernorm(x, axis=-1), L0_attn_Wq, L0_attn_Wk, L0_attn_Wv, L0_attn_Wo)
    x = x + _L0_ffn_ref(_layernorm(x, axis=-1), L0_ffn_gate_w, L0_ffn_w1, L0_ffn_w2)
    return x

_drawn_inputs = setup_inputs


def setup_inputs(seed=0):
    import zlib

    import numpy as np

    out = dict(_drawn_inputs(seed))
    spreads = {}
    factors = {'L0_ffn_gate_w': 5.358, 'L0_ffn_w1': 4.79, 'L0_ffn_w2': 4.711}
    for name, (base, spread) in spreads.items():
        noise = np.random.default_rng([zlib.crc32(name.encode()), seed]).standard_normal(out[name].shape)
        drawn = base * np.exp(spread * noise) if base else spread * noise
        out[name] = jnp.asarray(drawn.astype(out[name].dtype))
    for name, factor in factors.items():
        out[name] = (out[name] * factor).astype(out[name].dtype)
    return out
```

```python
import numpy as np
import concourse.bass as bass
from concourse import mybir
from contextlib import ExitStack

F32 = mybir.dt.float32
F32R = mybir.dt.float32r
BF16 = mybir.dt.bfloat16
ALU = mybir.AluOpType
ACT = mybir.ActivationFunctionType
AX = mybir.AxisListType

P = 128
B, T, D = 16, 256, 128
TB = T // P
H, DK, DV = 16, 8, 64
HG = 4
G = H // HG
ROWS = P // HG
UNITS = B * G
E, FF = 8, 512
CAP = 2 * T // E
HC = FF // P
EPS = 1e-5
MASKED = -1e30
RING = 2


def has(index, n):
    return not isinstance(index, int) or 0 <= index < n


def await_count(engine, sem, count):
    if not isinstance(count, int) or count > 0:
        engine.wait_ge(sem, count)


def bcast(ap, axis, n):
    ap = ap.unsqueeze(axis)
    shape = list(ap.shape)
    shape[axis] = n
    return ap.broadcast_to(shape)


def f32(ap):
    return ap.bitcast(F32)


def block_kernel(nc, x, w_q, w_k, w_v, w_o, gate_w, w1, w2, out):
    x_tiles = x.rearrange("b (t p) d -> p (b t) d", p=P)
    out_tiles = out.rearrange("b (t p) d -> p (b t) d", p=P)

    with ExitStack() as ctx:
        def sb(name, shape, dt=F32, scope=ctx):
            return scope.enter_context(nc.sbuf_tensor(name, shape, dt))

        def sem(name, scope=ctx):
            return scope.enter_context(nc.semaphore(name))

        x_all = sb("x_all", [P, B * TB, D])
        xg_hi = sb("xg_hi", [P, B * TB, D], F32R)
        xg_lo = sb("xg_lo", [P, B * TB, D], F32R)
        gate_logit = sb("gate_logit", [P, B * TB, E])
        ident = sb("ident", [P, P])
        w1_raw = sb("w1_raw", [P, E, FF])
        w2_sb = sb("w2_sb", [P, E, HC, D])
        experts_loaded = sem("experts_loaded")

        attention(nc, x_tiles, w_q, w_k, w_v, w_o, gate_w, w1, w2,
                  x_all, xg_hi, xg_lo, gate_logit, ident, w1_raw, w2_sb, experts_loaded)
        experts(nc, out_tiles, x_all, xg_hi, xg_lo, gate_logit, ident, w1_raw, w2_sb,
                experts_loaded)


def attention(nc, x_tiles, w_q, w_k, w_v, w_o, gate_w, w1, w2,
              x_all, xg_hi, xg_lo, gate_logit, ident, w1_raw, w2_sb, experts_loaded):
    with ExitStack() as ctx:
        def sb(name, shape, dt=F32):
            return ctx.enter_context(nc.sbuf_tensor(name, shape, dt))

        def ps(name, shape):
            return ctx.enter_context(nc.psum_tensor(name, shape, F32))

        def sem(name):
            return ctx.enter_context(nc.semaphore(name))

        wqk_raw = sb("wqk_raw", [P, 2, H * DK])
        wv_raw = sb("wv_raw", [P, H * DV])
        wqk_hi = sb("wqk_hi", [P, 2, H, 4, DK], F32R)
        wqk_lo = sb("wqk_lo", [P, 2, H, 4, DK], F32R)
        wv_hi = sb("wv_hi", [P, H * DV], F32R)
        wv_lo = sb("wv_lo", [P, H * DV], F32R)
        wo_sb = sb("wo_sb", [P, H * DV // P, D])
        gate_sb = sb("gate_sb", [P, E])
        ident_bf = sb("ident_bf", [P, P], BF16)
        causal = sb("causal", [P, P], BF16)
        neg_half = sb("neg_half", [P, TB])
        eps_sb = sb("eps_sb", [P, TB])
        low_row = sb("low_row", [P, 2, HG, 4, DK])
        low_diag = sb("low_diag", [P, 2, P])
        minus_low = sb("minus_low", [P, 2])
        holds_wait = sb("holds_wait", [P, 1])
        bn6 = sb("bn6", [P, TB, 6])
        mv1 = sb("mv1", [P, TB, 2])
        var1 = sb("var1", [P, TB])
        rstd1 = sb("rstd1", [P, TB])
        xn1 = sb("xn1", [P, TB, D])
        bn6b = sb("bn6b", [P, TB, 6])
        mv2 = sb("mv2", [P, TB, 2])
        var2 = sb("var2", [P, TB])
        rstd2 = sb("rstd2", [P, TB])
        xn2 = sb("xn2", [P, TB, D])
        xn2T = sb("xn2T", [P, T])
        xT_hi = [sb(f"xT_hi{r}", [P, T], F32R) for r in range(RING)]
        xT_lo = [sb(f"xT_lo{r}", [P, T], F32R) for r in range(RING)]
        v_sb = [sb(f"v_sb{r}", [P, TB, H * DV]) for r in range(RING)]
        ctxT = [sb(f"ctxT{r}", [P, H * DV // P, T]) for r in range(RING)]
        qk_hi = [sb(f"qk_hi{r}", [P, 2, T], F32R) for r in range(RING)]
        qT = [sb(f"qT{r}", [P, T], F32R) for r in range(RING)]
        k_diag = [sb(f"k_diag{r}", [P, HG, T], F32R) for r in range(RING)]
        neg_max = sb("neg_max", [P, RING, 2, HG])
        sums = sb("sums", [P, RING, 2, HG])
        inv = sb("inv", [P, RING, 2, HG])
        prob = [sb(f"prob{r}", [P, HG * 3 * P]) for r in range(RING)]
        probn = [sb(f"probn{r}", [P, HG * 3 * P]) for r in range(RING)]
        probT = [sb(f"probT{r}", [P, HG * 3 * P]) for r in range(RING)]

        s0_ps = ps("s0_ps", [P, HG, P])
        s1_ps = ps("s1_ps", [P, HG, T])
        t_ps = [ps(f"t_ps{r}", [P, 512]) for r in range(RING)]
        ctx_ps = ps("ctx_ps", [P, 2, T])
        misc_ps = [ps(f"misc_ps{r}", [P, 512]) for r in range(RING)]

        x_loaded = [sem(f"x_loaded{i}") for i in range(4)]
        wqk_loaded = sem("wqk_loaded")
        wv_loaded = sem("wv_loaded")
        wo_loaded = sem("wo_loaded")
        consts = sem("consts")
        consts2 = sem("consts2")
        low_rows = sem("low_rows")
        low_diags = sem("low_diags")
        lows_ready = sem("lows_ready")
        diag_zero = sem("diag_zero")
        w_hi = sem("w_hi")
        w_lo = sem("w_lo")
        bn1_done = sem("bn1_done")
        stats1 = sem("stats1")
        var1_done = sem("var1_done")
        rstd1_done = sem("rstd1_done")
        xn1_ready = sem("xn1_ready")
        xT_done = sem("xT_done")
        xT_hi_done = sem("xT_hi_done")
        xT_ready = sem("xT_ready")
        qk_done = sem("qk_done")
        qk_hi_done = sem("qk_hi_done")
        qk_ready = sem("qk_ready")
        v_done = sem("v_done")
        v_ready = sem("v_ready")
        s0_done = sem("s0_done")
        s1_done = sem("s1_done")
        max0 = sem("max0")
        max1 = sem("max1")
        exp0 = sem("exp0")
        exp1 = sem("exp1")
        inv0 = sem("inv0")
        inv1 = sem("inv1")
        normed = sem("normed")
        t_done = sem("t_done")
        t_act = sem("t_act")
        t_dve = sem("t_dve")
        ctx_done = sem("ctx_done")
        ctx_ready = sem("ctx_ready")
        wo_done = sem("wo_done")
        x1_ready = sem("x1_ready")
        bn2_done = sem("bn2_done")
        stats2 = sem("stats2")
        var2_done = sem("var2_done")
        rstd2_done = sem("rstd2_done")
        xn2_ready = sem("xn2_ready")
        x2T_done = sem("x2T_done")
        x2T_ready = sem("x2T_ready")
        xg_hi_done = sem("xg_hi_done")
        xg_lo_done = sem("xg_lo_done")
        gate_done = sem("gate_done")
        gate_ready = sem("gate_ready")

        XPART = B // 4

        def batches(engine, batch):
            for b in (-1, 0, 1):
                batch(b, b % 2)
            with engine.Fori(1, (B - 2) // 2) as pair:
                for k in range(2):
                    batch(pair * 2 + k, k)
            for b in (B - 2, B - 1, B, B + 1):
                batch(b, b % 2)

        block = ctx.enter_context(nc.Block())

        @block.sync
        def _(sp):
            sp.dma_start(x_all[:, 0:XPART * TB, :], x_tiles[:, 0:XPART * TB, :]).then_inc(x_loaded[0], 16)
            sp.dma_start(wqk_raw[:, 0, :], w_q).then_inc(wqk_loaded, 16)
            sp.dma_start(wqk_raw[:, 1, :], w_k).then_inc(wqk_loaded, 16)
            sp.dma_start(wv_raw[:, :], w_v).then_inc(wv_loaded, 16)
            sp.dma_start(wo_sb[:, :, :], w_o.rearrange("(c p) n -> p c n", p=P)).then_inc(wo_loaded, 16)
            sp.dma_start(gate_sb[:, :], gate_w).then_inc(wo_loaded, 16)
            for i in range(1, 4):
                part = slice(i * XPART * TB, (i + 1) * XPART * TB)
                sp.dma_start(x_all[:, part, :], x_tiles[:, part, :]).then_inc(x_loaded[i], 16)
            sp.dma_start(w1_raw[:, :, :], w1.rearrange("e c h -> c e h")).then_inc(experts_loaded, 16)
            sp.dma_start(w2_sb[:, :, :, :], w2.rearrange("e (k p) c -> p e k c", p=P)).then_inc(experts_loaded, 16)

        @block.gpsimd
        def _(pool):
            nc.gpsimd.memset(ident[:, :], 0.0).then_inc(consts, 1)
            nc.gpsimd.memset(ident_bf[:, :], 0.0).then_inc(consts, 1)
            nc.gpsimd.memset(causal[:, :], 0.0).then_inc(consts, 1)
            nc.gpsimd.memset(neg_half[:, :], -0.5)
            nc.gpsimd.memset(eps_sb[:, :], EPS).then_inc(consts, 1)
            pool.wait_ge(consts, 4)
            for m in (ident, ident_bf):
                nc.gpsimd.affine_select(out=m[:, :], in_=m[:, :], compare_op=ALU.not_equal, fill=1.0, base=0,
                                        pattern=[[-1, P]], channel_multiplier=1).then_inc(consts2, 1)
            nc.gpsimd.affine_select(out=causal[:, :], in_=causal[:, :], compare_op=ALU.is_ge, fill=MASKED,
                                    base=0, pattern=[[-1, P]], channel_multiplier=1).then_inc(consts2, 1)

            def batch(b, par):
                for j in range(G):
                    u, r = b * G + j, j % RING
                    if has(u, UNITS):
                        pool.wait_ge(inv0, u + 1)
                        await_count(pool, t_done, (u - 1) * 3)
                        nc.gpsimd.tensor_tensor(
                            probn[r][:, 0:HG * P].rearrange("p (i k) -> p i k", i=HG),
                            prob[r][:, 0:HG * P].rearrange("p (i k) -> p i k", i=HG),
                            bcast(inv[:, r, 0, :], 2, P), ALU.mult).then_inc(normed, 1)
                    if j == 0 and has(b + 1, B):
                        pool.wait_ge(stats1, b + 2)
                        nc.gpsimd.tensor_tensor(var1[:, :], mv1[:, :, 1], eps_sb[:, :], ALU.add).then_inc(var1_done, 1)
                        pool.wait_ge(var1_done, b + 2)
                        nc.gpsimd.tensor_tensor(rstd1[:, :], var1[:, :], neg_half[:, :], ALU.pow).then_inc(rstd1_done, 1)
                    if j == 3 and has(b - 1, B):
                        pool.wait_ge(stats2, b)
                        nc.gpsimd.tensor_tensor(var2[:, :], mv2[:, :, 1], eps_sb[:, :], ALU.add).then_inc(var2_done, 1)
                        pool.wait_ge(var2_done, b)
                        nc.gpsimd.tensor_tensor(rstd2[:, :], var2[:, :], neg_half[:, :], ALU.pow).then_inc(rstd2_done, 1)
                    if has(u, UNITS):
                        pool.wait_ge(inv1, u + 1)
                        nc.gpsimd.tensor_tensor(
                            probn[r][:, HG * P:].rearrange("p (i k) -> p i k", i=HG),
                            prob[r][:, HG * P:].rearrange("p (i k) -> p i k", i=HG),
                            bcast(inv[:, r, 1, :], 2, T), ALU.mult).then_inc(normed, 1)

            batches(pool, batch)

        @block.scalar
        def _(act):
            act.wait_ge(wqk_loaded, 32)
            for w in range(2):
                nc.scalar.activation(wqk_hi[:, w, :, :, :],
                                     bcast(wqk_raw[:, w, :].rearrange("p (h d) -> p h d", h=H), 2, 4),
                                     ACT.Copy, scale=(DK ** -0.5 if w == 0 else 1.0)).then_inc(w_hi, 1)
            act.wait_ge(wv_loaded, 16)
            nc.scalar.activation(wv_hi[:, :], wv_raw[:, :], ACT.Copy).then_inc(w_hi, 1)

            def exps(w, r, block_, scores, keys, first, done):
                for i in range(HG):
                    last = nc.scalar.activation(
                        prob[r][:, first + i * keys:first + (i + 1) * keys], scores[:, i, :], ACT.Exp,
                        bias=neg_max[:, r, block_, i:i + 1], accum_out=sums[:, r, block_, i:i + 1])
                last.then_inc(done, 1)

            def batch(b, par):
                for j in range(G):
                    u = b * G + j
                    r1, r2, rm = (j + 1) % RING, j % RING, (j + 1) % RING
                    if has(u + 1, UNITS):
                        act.wait_ge(max0, u + 2)
                        await_count(act, normed, u * 2)
                        exps(u + 1, r1, 0, s0_ps, P, 0, exp0)
                    if has(u + 2, UNITS):
                        act.wait_ge(qk_done, u + 3)
                        await_count(act, qk_ready, u + 1)
                        nc.scalar.activation(qk_hi[r2][:, :, :],
                                             misc_ps[(3 * j) % 2][:, :].rearrange("p (a t) -> p a t", a=2),
                                             ACT.Copy).then_inc(qk_hi_done, 1)
                    if has(u - 1, UNITS):
                        act.wait_ge(t_done, (u - 1) * 3 + 1)
                        await_count(act, ctx_done, u - 2)
                        nc.scalar.activation(probT[rm][:, 0:512], t_ps[rm][:, :], ACT.Copy).then_inc(t_act, 1)
                    if has(u + 1, UNITS):
                        act.wait_ge(max1, u + 2)
                        exps(u + 1, r1, 1, s1_ps, T, HG * P, exp1)
                    if has(u - 1, UNITS):
                        act.wait_ge(t_done, (u - 1) * 3 + 2)
                        nc.scalar.activation(probT[rm][:, 512:1024], t_ps[1 - rm][:, :], ACT.Copy).then_inc(t_act, 1)
                    if has(u + 2, UNITS):
                        w, q = u + 2, (j + 2) % G
                        vb = par if j < 2 else 1 - par
                        act.wait_ge(v_done, w + 1)
                        await_count(act, ctx_done, w - q - G)
                        nc.scalar.activation(v_sb[vb][:, q % 2, (q // 2) * 512:(q // 2 + 1) * 512],
                                             misc_ps[(3 * j + 1) % 2][:, :], ACT.Copy).then_inc(v_ready, 1)
                    if j == 0 and has(b - 2, B):
                        act.wait_ge(xn2_ready, b - 1)
                        nc.scalar.activation(xg_hi[:, bass.ds((b - 2) * TB, TB), :], xn2[:, :, :],
                                             ACT.Copy).then_inc(xg_hi_done, 1)
                    if j == 1 and has(b + 1, B):
                        act.wait_ge(xT_done, b + 2)
                        nc.scalar.activation(xT_hi[1 - par][:, :], misc_ps[(3 * j + 2) % 2][:, 0:T],
                                             ACT.Copy).then_inc(xT_hi_done, 1)

            batches(act, batch)

        @block.vector
        def _(dve):
            nc.vector.memset(low_row[:, :, :, :, :], 0.0).then_inc(low_rows, 1)
            dve.wait_ge(low_rows, 1)
            nc.vector.memset(low_row[:, 0, :, 2:4, :], -1.0)
            nc.vector.memset(low_row[:, 1, :, 1, :], -1.0)
            nc.vector.memset(low_row[:, 1, :, 3, :], -1.0).then_inc(low_rows, 1)
            dve.wait_ge(low_rows, 2)
            dve.wait_ge(consts2, 3)
            nc.vector.tensor_tensor(low_diag[:, :, :], low_row[:, :, :, :, :].rearrange("p a i r d -> p a (i r d)"),
                                    bcast(ident[:, :], 1, 2), ALU.mult).then_inc(low_diags, 1)
            dve.wait_ge(low_diags, 1)
            nc.vector.tensor_reduce(out=minus_low[:, :], in_=low_diag[:, :, :], axis=AX.X,
                                    op=ALU.add).then_inc(lows_ready, 1)
            for r in range(RING):
                nc.vector.memset(f32(k_diag[r][:, :, :]), 0.0).then_inc(diag_zero, 1)
            dve.wait_ge(lows_ready, 1)
            dve.wait_ge(diag_zero, RING)
            dve.wait_ge(w_hi, 2)
            nc.vector.scalar_tensor_tensor(
                out=wqk_lo[:, 0, :, 0, :],
                in0=wqk_raw[:, 0, :].rearrange("p (h d) -> p h d", h=H), scalar=DK ** -0.5,
                in1=f32(wqk_hi[:, 0, :, 0, :]), op0=ALU.mult, op1=ALU.subtract).then_inc(w_lo, 1)
            nc.vector.tensor_tensor(wqk_lo[:, 1, :, 0, :], wqk_raw[:, 1, :].rearrange("p (h d) -> p h d", h=H),
                                    f32(wqk_hi[:, 1, :, 0, :]), ALU.subtract).then_inc(w_lo, 1)
            dve.wait_ge(w_lo, 2)
            for w in range(2):
                nc.vector.tensor_copy(wqk_lo[:, w, :, 1:4, :], bcast(f32(wqk_lo[:, w, :, 0, :]), 2, 3)).then_inc(w_lo, 1)
            dve.wait_ge(w_hi, 3)
            nc.vector.tensor_tensor(wv_lo[:, :], wv_raw[:, :], f32(wv_hi[:, :]), ALU.subtract).then_inc(w_lo, 1)

            def norm_stats(src, bn, mv, bn_done, bn_count, stats_done):
                nc.vector.memset(holds_wait[:, :], 0.0)
                for tb in range(TB):
                    last = nc.vector.bn_stats(bn[:, tb, :], src(tb))
                last.then_inc(bn_done, 1)
                dve.wait_ge(bn_done, bn_count)
                nc.vector.memset(holds_wait[:, :], 0.0)
                for tb in range(TB):
                    last = nc.vector.bn_aggr(mv[:, tb, :], bn[:, tb, :])
                last.then_inc(stats_done, 1)

            def batch(b, par):
                for j in range(G):
                    u = b * G + j
                    r1, r2, rm = (j + 1) % RING, j % RING, (j + 1) % RING
                    if has(u + 1, UNITS):
                        dve.wait_ge(s0_done, u + 2)
                        nc.vector.tensor_reduce(out=neg_max[:, r1, 0, :], in_=s0_ps[:, :, :], axis=AX.X,
                                                op=ALU.max, negate=True).then_inc(max0, 1)
                    if j == 0 and has(b + 1, B):
                        if isinstance(b, int) and b < 0:
                            dve.wait_ge(x_loaded[0], 16)
                        if isinstance(b, int) and b == 1:
                            for i in range(1, 4):
                                dve.wait_ge(x_loaded[i], 16)
                        await_count(dve, rstd1_done, b + 1)
                        norm_stats(lambda tb: x_all[:, (b + 1) * TB + tb, :], bn6, mv1, bn1_done, b + 2, stats1)
                    if has(u + 2, UNITS):
                        w = u + 2
                        qk_ps = misc_ps[(3 * j) % 2][:, :].rearrange("p (a t) -> p a t", a=2)
                        dve.wait_ge(qk_hi_done, w + 1)
                        await_count(dve, s1_done, w - 1)
                        nc.vector.scalar_tensor_tensor(out=qT[r2][:, :], in0=f32(qk_hi[r2][:, 0, :]),
                                                       scalar=minus_low[:, 0:1], in1=qk_ps[:, 0, :],
                                                       op0=ALU.mult, op1=ALU.add)
                        for i in range(HG):
                            rows = slice(i * ROWS, (i + 1) * ROWS)
                            last = nc.vector.scalar_tensor_tensor(
                                out=k_diag[r2][rows, i, :], in0=f32(qk_hi[r2][rows, 1, :]),
                                scalar=minus_low[rows, 1:2], in1=qk_ps[rows, 1, :], op0=ALU.mult, op1=ALU.add)
                        last.then_inc(qk_ready, 1)
                    if has(u + 1, UNITS):
                        dve.wait_ge(s1_done, u + 2)
                        nc.vector.tensor_reduce(out=neg_max[:, r1, 1, :], in_=s1_ps[:, :, :], axis=AX.X,
                                                op=ALU.max, negate=True).then_inc(max1, 1)
                        dve.wait_ge(exp0, u + 2)
                        nc.vector.reciprocal(inv[:, r1, 0, :], sums[:, r1, 0, :]).then_inc(inv0, 1)
                    if j == 1 and has(b + 1, B):
                        dve.wait_ge(rstd1_done, b + 2)
                        await_count(dve, xT_done, b + 1)
                        for tb in range(TB):
                            last = nc.vector.tensor_scalar(xn1[:, tb, :], x_all[:, (b + 1) * TB + tb, :],
                                                           mv1[:, tb, 0:1], rstd1[:, tb:tb + 1],
                                                           ALU.subtract, ALU.mult)
                        last.then_inc(xn1_ready, 1)
                    if has(u - 1, UNITS):
                        dve.wait_ge(t_done, (u - 1) * 3 + 3)
                        await_count(dve, ctx_done, u - 2)
                        nc.vector.tensor_copy(probT[rm][:, 1024:1536], t_ps[rm][:, :]).then_inc(t_dve, 1)
                    if has(u - 2, UNITS):
                        cb = par if j >= 2 else 1 - par
                        g = (j - 2) % G
                        dve.wait_ge(ctx_done, u - 1)
                        await_count(dve, wo_done, b - 1 if j >= 2 else b - 2)
                        nc.vector.tensor_copy(ctxT[cb][:, 2 * g:2 * g + 2, :], ctx_ps[:, :, :]).then_inc(ctx_ready, 1)
                    if has(u + 1, UNITS):
                        dve.wait_ge(exp1, u + 2)
                        nc.vector.reciprocal(inv[:, r1, 1, :], sums[:, r1, 1, :]).then_inc(inv1, 1)
                    extra = misc_ps[(3 * j + 2) % 2]
                    if j == 0 and has(b - 2, B):
                        dve.wait_ge(x2T_done, b - 1)
                        await_count(dve, gate_done, b - 2)
                        nc.vector.tensor_copy(xn2T[:, :], extra[:, 0:T]).then_inc(x2T_ready, 1)
                        dve.wait_ge(xg_hi_done, b - 1)
                        tiles = bass.ds((b - 2) * TB, TB)
                        nc.vector.tensor_tensor(xg_lo[:, tiles, :], xn2[:, :, :], f32(xg_hi[:, tiles, :]),
                                                ALU.subtract).then_inc(xg_lo_done, 1)
                    if j == 1 and has(b + 1, B):
                        dve.wait_ge(xT_hi_done, b + 2)
                        nc.vector.tensor_tensor(xT_lo[1 - par][:, :], extra[:, 0:T], f32(xT_hi[1 - par][:, :]),
                                                ALU.subtract).then_inc(xT_ready, 1)
                    if j == 2 and has(b - 1, B):
                        tiles = bass.ds((b - 1) * TB, TB)
                        dve.wait_ge(wo_done, b)
                        nc.vector.tensor_tensor(x_all[:, tiles, :], extra[:, 0:T].rearrange("p (t d) -> p t d", t=TB),
                                                x_all[:, tiles, :], ALU.add).then_inc(x1_ready, 1)
                        dve.wait_ge(x1_ready, b)
                        await_count(dve, rstd2_done, b - 1)
                        norm_stats(lambda tb: x_all[:, (b - 1) * TB + tb, :], bn6b, mv2, bn2_done, b, stats2)
                    if j == 3 and has(b - 2, B):
                        dve.wait_ge(gate_done, b - 1)
                        nc.vector.tensor_copy(gate_logit[:, bass.ds((b - 2) * TB, TB), :],
                                              extra[:, 0:TB * E].rearrange("p (t e) -> p t e", t=TB)).then_inc(gate_ready, 1)
                    if j == 3 and has(b - 1, B):
                        dve.wait_ge(rstd2_done, b)
                        await_count(dve, x2T_done, b - 1)
                        await_count(dve, xg_lo_done, b - 1)
                        for tb in range(TB):
                            last = nc.vector.tensor_scalar(xn2[:, tb, :], x_all[:, (b - 1) * TB + tb, :],
                                                           mv2[:, tb, 0:1], rstd2[:, tb:tb + 1],
                                                           ALU.subtract, ALU.mult)
                        last.then_inc(xn2_ready, 1)

            batches(dve, batch)

        @block.tensor
        def _(pe):
            pe.wait_ge(consts2, 3)
            pe.wait_ge(w_hi, 3)
            pe.wait_ge(w_lo, 5)
            pe.wait_ge(wo_loaded, 32)

            def split_product(out_, w_h, w_l, x_h, x_l):
                nc.tensor.matmul(out_, w_h, x_h, start=True, stop=False)
                nc.tensor.matmul(out_, w_h, x_l, start=False, stop=False)
                return nc.tensor.matmul(out_, w_l, x_h, start=False, stop=True)

            def batch(b, par):
                for j in range(G):
                    u = b * G + j
                    r1, r2, rm = (j + 1) % RING, j % RING, (j + 1) % RING
                    if has(u + 1, UNITS):
                        pe.wait_ge(qk_ready, u + 2)
                        await_count(pe, exp0, u + 1)
                        nc.tensor.matmul(s0_ps[:, :, :], qT[r1][:, 0:P], k_diag[r1][:, :, 0:P], start=True, stop=False)
                        nc.tensor.matmul(s0_ps[:, :, :], ident_bf[:, :], bcast(causal[:, :], 1, HG),
                                         start=False, stop=True).then_inc(s0_done, 1)
                    if has(u + 2, UNITS):
                        w, g = u + 2, (j + 2) % G
                        xb = par if j < 2 else 1 - par
                        heads = slice(g * HG, (g + 1) * HG)
                        qk_ps = misc_ps[(3 * j) % 2]
                        pe.wait_ge(xT_ready, b + 1 if j < 2 else b + 2)
                        await_count(pe, v_ready, w)
                        for a in range(2):
                            last = split_product(qk_ps[:, a * T:(a + 1) * T],
                                                 wqk_hi[:, a, heads, :, :].rearrange("p h r d -> p (h r d)"),
                                                 wqk_lo[:, a, heads, :, :].rearrange("p h r d -> p (h r d)"),
                                                 xT_hi[xb][:, :], xT_lo[xb][:, :])
                        last.then_inc(qk_done, 1)
                    if has(u + 1, UNITS):
                        await_count(pe, exp1, u + 1)
                        for i in (0, 2):
                            nc.tensor.matmul(s1_ps[:, i:i + 2, :], qT[r1][:, P:T], k_diag[r1][:, i:i + 2, :],
                                             start=True, stop=False)
                            last = nc.tensor.matmul(s1_ps[:, i:i + 2, P:T], ident_bf[:, :], bcast(causal[:, :], 1, 2),
                                                    start=False, stop=True)
                        last.then_inc(s1_done, 1)
                    if has(u - 1, UNITS):
                        w = u - 1
                        pe.wait_ge(normed, w * 2 + 2)
                        q0 = probn[rm][:, 0:HG * P].rearrange("p (i k) -> p i k", i=HG)
                        q1 = probn[rm][:, HG * P:].rearrange("p (i k) -> p i k", i=HG)
                        for f in range(2):
                            await_count(pe, *((t_act, w * 2) if f == 0 else (t_dve, w)))
                            t = t_ps[rm if f == 0 else 1 - rm][:, :].rearrange("p (i q) -> p i q", i=2)
                            for i in range(2):
                                nc.tensor.transpose(t[:, i, 0:P], q0[:, 2 * f + i, :], ident[:, :])
                                last = nc.tensor.transpose(t[:, i, P:T], q1[:, 2 * f + i, 0:P], ident[:, :])
                            last.then_inc(t_done, 1)
                    if has(u + 2, UNITS):
                        w, q = u + 2, (j + 2) % G
                        xb = par if j < 2 else 1 - par
                        await_count(pe, *[(gate_ready, b - 2), (x2T_ready, b - 1), (xT_ready, b + 2),
                                          (x1_ready, b)][j])
                        toks = slice((q % 2) * P, (q % 2 + 1) * P)
                        cols = slice((q // 2) * 512, (q // 2 + 1) * 512)
                        split_product(misc_ps[(3 * j + 1) % 2][:, :], xT_hi[xb][:, toks], xT_lo[xb][:, toks],
                                      wv_hi[:, cols], wv_lo[:, cols]).then_inc(v_done, 1)
                    if has(u - 1, UNITS):
                        w = u - 1
                        pe.wait_ge(t_act, w * 2 + 1)
                        t = t_ps[rm][:, :].rearrange("p (i q) -> p i q", i=HG)
                        for i in range(HG):
                            last = nc.tensor.transpose(t[:, i, :], q1[:, i, P:T], ident[:, :])
                        last.then_inc(t_done, 1)
                    if has(u - 2, UNITS):
                        w, g = u - 2, (j - 2) % G
                        vb = par if j >= 2 else 1 - par
                        pe.wait_ge(t_act, w * 2 + 2)
                        pe.wait_ge(t_dve, w + 1)
                        pe.wait_ge(v_ready, w - g + 2 * (g // 2) + 2)
                        await_count(pe, ctx_ready, w)
                        pt = probT[r2]
                        for pair in range(2):
                            for kb in range(TB):
                                for half in range(2):
                                    i = 2 * pair + half
                                    h = g * HG + i
                                    rhs = (pt[:, i * T:(i + 1) * T] if kb == 0 else
                                           pt[:, HG * T + i * P:HG * T + (i + 1) * P])
                                    last = nc.tensor.matmul(ctx_ps[half * DV:(half + 1) * DV, pair, kb * P:T],
                                                            v_sb[vb][:, kb, h * DV:(h + 1) * DV], rhs,
                                                            start=(kb == 0), stop=(kb == 1))
                        last.then_inc(ctx_done, 1)
                    extra = misc_ps[(3 * j + 2) % 2]
                    if has(u + 2, UNITS) or not isinstance(b, int):
                        pe.wait_ge(qk_ready, u + 3)
                    if j == 0 and has(b - 2, B):
                        pe.wait_ge(xn2_ready, b - 1)
                        pe.wait_ge(x1_ready, b - 1)
                        for tb in range(TB):
                            last = nc.tensor.transpose(extra[:, tb * P:(tb + 1) * P], xn2[:, tb, :], ident[:, :])
                        last.then_inc(x2T_done, 1)
                    if j == 1 and has(b + 1, B):
                        pe.wait_ge(xn1_ready, b + 2)
                        for tb in range(TB):
                            last = nc.tensor.transpose(extra[:, tb * P:(tb + 1) * P], xn1[:, tb, :], ident[:, :])
                        last.then_inc(xT_done, 1)
                    if j == 2 and has(b - 1, B):
                        pe.wait_ge(ctx_ready, b * G)
                        await_count(pe, x2T_ready, b - 1)
                        chunks = H * DV // P
                        for tb in range(TB):
                            for c in range(chunks):
                                last = nc.tensor.matmul(extra[:, tb * D:(tb + 1) * D],
                                                        ctxT[1 - par][:, c, tb * P:(tb + 1) * P], wo_sb[:, c, :],
                                                        start=(c == 0), stop=(c == chunks - 1))
                        last.then_inc(wo_done, 1)
                    if j == 3 and has(b - 2, B):
                        pe.wait_ge(x2T_ready, b - 1)
                        await_count(pe, gate_ready, b - 2)
                        for tb in range(TB):
                            last = nc.tensor.matmul(extra[:, tb * E:(tb + 1) * E], xn2T[:, tb * P:(tb + 1) * P],
                                                    gate_sb[:, :], start=True, stop=True)
                        last.then_inc(gate_done, 1)

            batches(pe, batch)


def experts(nc, out_tiles, x_all, xg_hi, xg_lo, gate_logit, ident, w1_raw, w2_sb, experts_loaded):
    with ExitStack() as ctx:
        def sb(name, shape, dt=F32):
            return ctx.enter_context(nc.sbuf_tensor(name, shape, dt))

        def ps(name, shape):
            return ctx.enter_context(nc.psum_tensor(name, shape, F32))

        def sem(name):
            return ctx.enter_context(nc.semaphore(name))

        TILES = B * TB
        EP = E // 2
        QB = 4
        STEPS = range(-4, B + 6)

        w1_hi = sb("w1_hi", [P, E, FF], F32R)
        w1_lo = sb("w1_lo", [P, E, FF], F32R)
        neg_top = sb("neg_top", [P, TILES])
        shifted = sb("shifted", [P, TILES, E])
        weight = sb("weight", [P, TILES, E])
        total = sb("total", [P, TILES])
        inv_total = sb("inv_total", [P, TILES])
        probs = sb("probs", [P, TB, B, E])
        left = sb("left", [P, T])
        top8 = sb("top8", [P, CAP // 8, 8])
        taken = sb("taken", [P, T])
        zeros = sb("zeros", [P, T])
        running = sb("running", [P, T])
        slot_of = sb("slot_of", [P, T])
        slotT = sb("slotT", [P, TB, B, E])
        slot_no = sb("slot_no", [P, CAP])
        pick = [sb(f"pick{r}", [P, TB, E * CAP], F32R) for r in range(RING)]
        xin_hi = [sb(f"xin_hi{r}", [P, E, QB, CAP], F32R) for r in range(RING)]
        xin_lo = [sb(f"xin_lo{r}", [P, E, QB, CAP], F32R) for r in range(RING)]
        hT = [sb(f"hT{r}", [P, 2, HC, QB * CAP]) for r in range(RING)]
        y_sb = [sb(f"y_sb{r}", [P, QB, EP, D]) for r in range(RING)]
        put = [w1_raw[:, r * TB:(r + 1) * TB, :] for r in range(RING)]
        putT = [sb(f"putT{r}", [P, EP, T]) for r in range(RING)]

        pick_hi_ps = ps("pick_hi_ps", [P, E, CAP])
        pick_lo_ps = ps("pick_lo_ps", [P, E, CAP])
        h_ps = [ps(f"h_ps{r}", [P, 2, QB * CAP]) for r in range(RING)]
        y_ps = ps("y_ps", [P, QB, D])
        putT_ps = ps("putT_ps", [P, EP, T])
        out_ps = ps("out_ps", [P, TB, D])

        numbered = sem("numbered")
        route = sem("route")
        weight_done = sem("weight_done")
        probsT_done = sem("probsT_done")
        rounds = sem("rounds")
        slots_done = sem("slots_done")
        slotT_done = sem("slotT_done")
        slotT_ready = sem("slotT_ready")
        w1_hi_done = sem("w1_hi_done")
        w1_ready = sem("w1_ready")
        pick_ready = sem("pick_ready")
        pick_done = sem("pick_done")
        xin_hi_ready = sem("xin_hi_ready")
        xin_lo_ready = sem("xin_lo_ready")
        h_done = sem("h_done")
        h_ready = sem("h_ready")
        y_done = sem("y_done")
        y_ready = sem("y_ready")
        put_ready = sem("put_ready")
        putT_done = sem("putT_done")
        putT_ready = sem("putT_ready")
        out_done = sem("out_done")
        out_ready = sem("out_ready")
        stored = sem("stored")

        block = ctx.enter_context(nc.Block())

        @block.sync
        def _(sp):
            with sp.Fori(0, B) as b:
                sp.wait_ge(out_ready, b + 1)
                sp.dma_start(out_tiles[:, bass.ds(b * TB, TB), :], x_all[:, bass.ds(b * TB, TB), :]).then_inc(stored, 16)
            sp.wait_ge(stored, 16 * B)

        @block.gpsimd
        def _(pool):
            nc.gpsimd.iota(slot_no[:, :], pattern=[[1, CAP]], base=1, channel_multiplier=0,
                           allow_small_or_imprecise_dtypes=True).then_inc(numbered, 1)
            nc.gpsimd.memset(zeros[:, :], 0.0).then_inc(numbered, 1)

        @block.scalar
        def _(act):
            act.wait_ge(route, 2)
            nc.scalar.activation(weight[:, :, :], shifted[:, :, :], ACT.Exp).then_inc(weight_done, 1)
            act.wait_ge(experts_loaded, 32)
            nc.scalar.activation(w1_hi[:, :, :], w1_raw[:, :, :], ACT.Copy).then_inc(w1_hi_done, 1)
            for n in STEPS:
                b = n + 4
                if has(b, B):
                    act.wait_ge(pick_done, b + 1)
                    await_count(act, h_done, (b // QB - 1) * 16)
                    nc.scalar.activation(xin_hi[b // QB % RING][:, :, b % QB, :], pick_hi_ps[:, :, :],
                                         ACT.Copy).then_inc(xin_hi_ready, 1)
                if has(n, B):
                    await_count(act, y_done, n - 1)
                    for k in range(4):
                        act.wait_ge(h_done, 4 * n + k + 1)
                        nc.scalar.activation(hT[n % RING][:, k // 2, 2 * (k % 2):2 * (k % 2) + 2, :],
                                             h_ps[k % 2][:, :, :], ACT.Gelu).then_inc(h_ready, 1)
                b = n - 5
                if has(b, B):
                    act.wait_ge(putT_done, b + 1)
                    await_count(act, out_done, b - 1)
                    nc.scalar.activation(putT[b % RING][:, :, :], putT_ps[:, :, :], ACT.Copy).then_inc(putT_ready, 1)

        @block.vector
        def _(dve):
            nc.vector.tensor_reduce(out=neg_top[:, :], in_=gate_logit[:, :, :], axis=AX.X, op=ALU.max,
                                    negate=True).then_inc(route, 1)
            dve.wait_ge(route, 1)
            nc.vector.tensor_tensor(shifted[:, :, :], gate_logit[:, :, :], bcast(neg_top[:, :], 2, E),
                                    ALU.add).then_inc(route, 1)
            dve.wait_ge(weight_done, 1)
            nc.vector.tensor_reduce(out=total[:, :], in_=weight[:, :, :], axis=AX.X, op=ALU.add).then_inc(route, 1)
            dve.wait_ge(route, 3)
            nc.vector.reciprocal(inv_total[:, :], total[:, :]).then_inc(route, 1)
            dve.wait_ge(route, 4)
            for tb in range(TB):
                last = nc.vector.tensor_tensor(
                    probs[:, tb, :, :], weight[:, :, :].rearrange("p (b t) e -> p t b e", t=TB)[:, tb, :, :],
                    bcast(inv_total[:, :].rearrange("p (b t) -> p t b", t=TB)[:, tb, :], 2, E), ALU.mult)
            last.then_inc(route, 1)
            dve.wait_ge(probsT_done, 1)
            nc.vector.tensor_copy(left[:, :], h_ps[0][:, 0, :]).then_inc(rounds, 1)
            for k in range(CAP // 8):
                dve.wait_ge(rounds, 2 * k + 1)
                nc.vector.max(out=top8[:, k, :], in_=left[:, :]).then_inc(rounds, 1)
                dve.wait_ge(rounds, 2 * k + 2)
                nc.vector.match_replace(out=left[:, :], in_to_replace=top8[:, k, :], in_values=left[:, :],
                                        imm_value=-1.0).then_inc(rounds, 1)
            dve.wait_ge(rounds, 2 * (CAP // 8) + 1)
            nc.vector.tensor_scalar(taken[:, :], left[:, :], 0.0, None, ALU.is_lt).then_inc(slots_done, 1)
            dve.wait_ge(slots_done, 1)
            dve.wait_ge(numbered, 2)
            nc.vector.tensor_tensor_scan(running[:, :], taken[:, :], zeros[:, :], 0.0, ALU.add, ALU.add).then_inc(slots_done, 1)
            dve.wait_ge(slots_done, 2)
            nc.vector.tensor_tensor(slot_of[:, :], running[:, :], taken[:, :], ALU.mult).then_inc(slots_done, 1)
            dve.wait_ge(slotT_done, 1)
            nc.vector.tensor_copy(slotT[:, :, :, :].rearrange("p t b e -> p t (b e)"),
                                  h_ps[1][:, 0, :].rearrange("p (t n) -> p t n", t=TB)).then_inc(slotT_ready, 1)
            dve.wait_ge(slotT_ready, 1)

            def picks(b):
                if has(b, B):
                    await_count(dve, pick_done, b - 1)
                    for tb in range(TB):
                        last = nc.vector.tensor_tensor(
                            pick[b % RING][:, tb, :].rearrange("p (e s) -> p e s", e=E),
                            bcast(slot_no[:, :], 1, E), bcast(slotT[:, tb, b, :], 2, CAP), ALU.is_equal)
                    last.then_inc(pick_ready, 1)

            picks(0)
            for n in STEPS:
                picks(n + 5)
                b = n + 4
                if has(b, B):
                    dve.wait_ge(pick_done, b + 1)
                    await_count(dve, h_done, (b // QB - 1) * 16)
                    nc.vector.tensor_copy(xin_lo[b // QB % RING][:, :, b % QB, :], pick_lo_ps[:, :, :]).then_inc(xin_lo_ready, 1)
                if n == -4:
                    dve.wait_ge(w1_hi_done, 1)
                    nc.vector.tensor_tensor(w1_lo[:, :, :], w1_raw[:, :, :], f32(w1_hi[:, :, :]), ALU.subtract).then_inc(w1_ready, 1)
                m = n - 1
                if has(m, B):
                    dve.wait_ge(y_done, m + 1)
                    await_count(dve, out_done, (m // QB - 1) * QB)
                    nc.vector.tensor_copy(y_sb[m // QB % RING][:, :, m % EP, :], y_ps[:, :, :]).then_inc(y_ready, 1)
                b = n - 4
                if has(b, B):
                    if b == 0:
                        dve.wait_ge(w1_ready, 1)
                    await_count(dve, putT_done, b - 1)
                    for tb in range(TB):
                        for e in range(E):
                            last = nc.vector.tensor_scalar(
                                put[b % RING][:, tb, e * CAP:(e + 1) * CAP], slot_no[:, :],
                                slotT[:, tb, b, e:e + 1], probs[:, tb, b, e:e + 1], ALU.is_equal, ALU.mult)
                    last.then_inc(put_ready, 1)
                b = n - 6
                if has(b, B):
                    dve.wait_ge(out_done, b + 1)
                    nc.vector.tensor_tensor(x_all[:, b * TB:(b + 1) * TB, :], out_ps[:, :, :],
                                            x_all[:, b * TB:(b + 1) * TB, :], ALU.add).then_inc(out_ready, 1)

        @block.tensor
        def _(pe):
            pe.wait_ge(route, 5)
            for tb in range(TB):
                last = nc.tensor.transpose(h_ps[0][:, 0, tb * P:(tb + 1) * P], probs[:, tb, :, :].rearrange("p b e -> p (b e)"), ident[:, :])
            last.then_inc(probsT_done, 1)
            pe.wait_ge(slots_done, 3)
            for tb in range(TB):
                last = nc.tensor.transpose(h_ps[1][:, 0, tb * P:(tb + 1) * P], slot_of[:, tb * P:(tb + 1) * P], ident[:, :])
            last.then_inc(slotT_done, 1)
            pe.wait_ge(slotT_ready, 1)
            for n in STEPS:
                b = n + 4
                if has(b, B):
                    pe.wait_ge(pick_ready, b + 1)
                    await_count(pe, xin_hi_ready, b)
                    await_count(pe, xin_lo_ready, b)
                    for part, to in ((xg_hi, pick_hi_ps), (xg_lo, pick_lo_ps)):
                        for tb in range(TB):
                            last = nc.tensor.matmul(to[:, :, :], part[:, b * TB + tb, :], pick[b % RING][:, tb, :],
                                                    start=(tb == 0), stop=(tb == TB - 1))
                    last.then_inc(pick_done, 1)
                if has(n, B):
                    if n == 0:
                        pe.wait_ge(w1_ready, 1)
                    quarter = n // QB
                    pe.wait_ge(xin_hi_ready, (quarter + 1) * QB)
                    pe.wait_ge(xin_lo_ready, (quarter + 1) * QB)
                    for k in range(4):
                        e = 2 * (n % EP) + k // 2
                        await_count(pe, h_ready, 4 * n + k - 1)
                        for c in range(2):
                            hidden = slice((2 * (k % 2) + c) * P, (2 * (k % 2) + c + 1) * P)
                            xh = xin_hi[quarter % RING][:, e, :, :].rearrange("p b s -> p (b s)")
                            xl = xin_lo[quarter % RING][:, e, :, :].rearrange("p b s -> p (b s)")
                            to = h_ps[k % 2][:, c, :]
                            nc.tensor.matmul(to, w1_hi[:, e, hidden], xh, start=True, stop=False)
                            nc.tensor.matmul(to, w1_hi[:, e, hidden], xl, start=False, stop=False)
                            last = nc.tensor.matmul(to, w1_lo[:, e, hidden], xh, start=False, stop=True)
                        last.then_inc(h_done, 1)
                m = n - 1
                if has(m, B):
                    pe.wait_ge(h_ready, 4 * (m + 1))
                    await_count(pe, y_ready, m)
                    for q in range(QB):
                        for c in range(HC):
                            for half in range(2):
                                last = nc.tensor.matmul(y_ps[half * CAP:(half + 1) * CAP, q, :],
                                                        hT[m % RING][:, half, c, q * CAP:(q + 1) * CAP],
                                                        w2_sb[:, 2 * (m % EP) + half, c, :],
                                                        start=(c == 0), stop=(c == HC - 1))
                    last.then_inc(y_done, 1)
                b = n - 5
                if has(b, B):
                    pe.wait_ge(put_ready, b + 1)
                    await_count(pe, putT_ready, b)
                    for ep in range(EP):
                        for tb in range(TB):
                            last = nc.tensor.transpose(putT_ps[:, ep, tb * P:(tb + 1) * P],
                                                       put[b % RING][:, tb, ep * P:(ep + 1) * P], ident[:, :])
                    last.then_inc(putT_done, 1)
                b = n - 6
                if has(b, B):
                    pe.wait_ge(putT_ready, b + 1)
                    pe.wait_ge(y_ready, (b // QB + 1) * EP)
                    await_count(pe, out_ready, b)
                    for tb in range(TB):
                        for ep in range(EP):
                            last = nc.tensor.matmul(out_ps[:, tb, :], putT[b % RING][:, ep, tb * P:(tb + 1) * P],
                                                    y_sb[b // QB % RING][:, b % QB, ep, :],
                                                    start=(ep == 0), stop=(ep == EP - 1))
                    last.then_inc(out_done, 1)


INPUTS = ["L0_attn_x", "L0_attn_Wq", "L0_attn_Wk", "L0_attn_Wv", "L0_attn_Wo",
          "L0_ffn_gate_w", "L0_ffn_w1", "L0_ffn_w2"]


def kernel(**inputs):
    import concourse.bacc as bacc
    from concourse.bass_utils import run_bass_kernel_spmd

    nc = bacc.Bacc("TRN2", target_bir_lowering=False, num_devices=1)
    arrays, aps = {}, []
    for name in INPUTS:
        a = np.ascontiguousarray(inputs[name])
        arrays[f"in_{name}"] = a
        aps.append(nc.dram_tensor(f"in_{name}", a.shape, mybir.dt.from_np(a.dtype), kind="ExternalInput").ap())
    result = nc.dram_tensor("out_0", [B, T, D], F32, kind="ExternalOutput").ap()
    block_kernel(nc, *aps, result)
    r = run_bass_kernel_spmd(nc, [arrays], core_ids=[0])
    return r.results[0]["out_0"]
```

```python
import numpy as np
import concourse.bass as bass
from concourse import mybir
from contextlib import ExitStack

F32 = mybir.dt.float32
F32R = mybir.dt.float32r
BF16 = mybir.dt.bfloat16
ALU = mybir.AluOpType
ACT = mybir.ActivationFunctionType
AX = mybir.AxisListType

P = 128
B, T, D = 16, 256, 128
TB = T // P
H, DK, DV = 16, 8, 64
HG = 4
G = H // HG
ROWS = P // HG
UNITS = B * G
E, FF = 8, 512
CAP = 2 * T // E
HC = FF // P
EPS = 1e-5
MASKED = -1e30
RING = 2


def has(index, n):
    return not isinstance(index, int) or 0 <= index < n


def await_count(engine, sem, count):
    if not isinstance(count, int) or count > 0:
        engine.wait_ge(sem, count)


def bcast(ap, axis, n):
    ap = ap.unsqueeze(axis)
    shape = list(ap.shape)
    shape[axis] = n
    return ap.broadcast_to(shape)


def f32(ap):
    return ap.bitcast(F32)


def block_kernel(nc, x, w_q, w_k, w_v, w_o, gate_w, w1, w2, out):
    x_tiles = x.rearrange("b (t p) d -> p (b t) d", p=P)
    out_tiles = out.rearrange("b (t p) d -> p (b t) d", p=P)

    with ExitStack() as ctx:
        def sb(name, shape, dt=F32, scope=ctx):
            return scope.enter_context(nc.sbuf_tensor(name, shape, dt))

        def sem(name, scope=ctx):
            return scope.enter_context(nc.semaphore(name))

        x_all = sb("x_all", [P, B * TB, D])
        xg_hi = sb("xg_hi", [P, B * TB, D], F32R)
        xg_lo = sb("xg_lo", [P, B * TB, D], F32R)
        gate_logit = sb("gate_logit", [P, B * TB, E])
        ident = sb("ident", [P, P])
        w1_raw = sb("w1_raw", [P, E, FF])
        w2_sb = sb("w2_sb", [P, E, HC, D])
        experts_loaded = sem("experts_loaded")

        attention(nc, x_tiles, w_q, w_k, w_v, w_o, gate_w, w1, w2,
                  x_all, xg_hi, xg_lo, gate_logit, ident, w1_raw, w2_sb, experts_loaded)
        experts(nc, out_tiles, x_all, xg_hi, xg_lo, gate_logit, ident, w1_raw, w2_sb,
                experts_loaded)


def attention(nc, x_tiles, w_q, w_k, w_v, w_o, gate_w, w1, w2,
              x_all, xg_hi, xg_lo, gate_logit, ident, w1_raw, w2_sb, experts_loaded):
    with ExitStack() as ctx:
        def sb(name, shape, dt=F32):
            return ctx.enter_context(nc.sbuf_tensor(name, shape, dt))

        def ps(name, shape):
            return ctx.enter_context(nc.psum_tensor(name, shape, F32))

        def sem(name):
            return ctx.enter_context(nc.semaphore(name))

        wqk_raw = sb("wqk_raw", [P, 2, H * DK])
        wv_raw = sb("wv_raw", [P, H * DV])
        wqk_hi = sb("wqk_hi", [P, 2, H, 4, DK], F32R)
        wqk_lo = sb("wqk_lo", [P, 2, H, 4, DK], F32R)
        wv_hi = sb("wv_hi", [P, H * DV], F32R)
        wv_lo = sb("wv_lo", [P, H * DV], F32R)
        wo_sb = sb("wo_sb", [P, H * DV // P, D])
        gate_sb = sb("gate_sb", [P, E])
        ident_bf = sb("ident_bf", [P, P], BF16)
        causal = sb("causal", [P, P], BF16)
        own_block = sb("own_block", [P, HG])
        neg_half = sb("neg_half", [P, TB])
        eps_sb = sb("eps_sb", [P, TB])
        low_row = sb("low_row", [P, 2, HG, 4, DK])
        low_diag = sb("low_diag", [P, 2, P])
        minus_low = sb("minus_low", [P, 2])
        holds_wait = sb("holds_wait", [P, 1])
        bn6 = sb("bn6", [P, TB, 6])
        mv1 = sb("mv1", [P, TB, 2])
        var1 = sb("var1", [P, TB])
        rstd1 = sb("rstd1", [P, TB])
        xn1 = sb("xn1", [P, TB, D])
        bn6b = sb("bn6b", [P, TB, 6])
        mv2 = sb("mv2", [P, TB, 2])
        var2 = sb("var2", [P, TB])
        rstd2 = sb("rstd2", [P, TB])
        xn2 = sb("xn2", [P, TB, D])
        xn2T = sb("xn2T", [P, T])
        xT_hi = [sb(f"xT_hi{r}", [P, T], F32R) for r in range(RING)]
        xT_lo = [sb(f"xT_lo{r}", [P, T], F32R) for r in range(RING)]
        v_sb = [sb(f"v_sb{r}", [P, TB, H * DV]) for r in range(RING)]
        ctxT = [sb(f"ctxT{r}", [P, H * DV // P, T]) for r in range(RING)]
        qk_hi = [sb(f"qk_hi{r}", [P, 2, T], F32R) for r in range(RING)]
        qT = [sb(f"qT{r}", [P, T], F32R) for r in range(RING)]
        kT = [sb(f"kT{r}", [P, T], F32R) for r in range(RING)]
        k_diag = [sb(f"k_diag{r}", [P, HG, T], F32R) for r in range(RING)]
        neg_max = sb("neg_max", [P, RING, 2, HG])
        sums = sb("sums", [P, RING, 2, HG])
        inv = sb("inv", [P, RING, 2, HG])
        prob = [sb(f"prob{r}", [P, HG * 3 * P]) for r in range(RING)]
        probn = [sb(f"probn{r}", [P, HG * 3 * P]) for r in range(RING)]
        probT = [sb(f"probT{r}", [P, HG * 3 * P]) for r in range(RING)]

        s0_ps = ps("s0_ps", [P, HG, P])
        s1_ps = ps("s1_ps", [P, HG, T])
        t_ps = [ps(f"t_ps{r}", [P, 512]) for r in range(RING)]
        ctx_ps = ps("ctx_ps", [P, 2, T])
        misc_ps = [ps(f"misc_ps{r}", [P, 512]) for r in range(RING)]

        x_loaded = [sem(f"x_loaded{i}") for i in range(4)]
        wqk_loaded = sem("wqk_loaded")
        wv_loaded = sem("wv_loaded")
        wo_loaded = sem("wo_loaded")
        consts = sem("consts")
        consts2 = sem("consts2")
        low_rows = sem("low_rows")
        low_diags = sem("low_diags")
        lows_ready = sem("lows_ready")
        w_hi = sem("w_hi")
        w_lo = sem("w_lo")
        bn1_done = sem("bn1_done")
        stats1 = sem("stats1")
        var1_done = sem("var1_done")
        rstd1_done = sem("rstd1_done")
        xn1_ready = sem("xn1_ready")
        xT_done = sem("xT_done")
        xT_hi_done = sem("xT_hi_done")
        xT_ready = sem("xT_ready")
        qk_done = sem("qk_done")
        qk_hi_done = sem("qk_hi_done")
        qk_ready = sem("qk_ready")
        k_ready = sem("k_ready")
        v_done = sem("v_done")
        v_ready = sem("v_ready")
        s0_done = sem("s0_done")
        s1_done = sem("s1_done")
        max0 = sem("max0")
        max1 = sem("max1")
        exp0 = sem("exp0")
        exp1 = sem("exp1")
        inv0 = sem("inv0")
        inv1 = sem("inv1")
        normed = sem("normed")
        t_done = sem("t_done")
        t_act = sem("t_act")
        t_dve = sem("t_dve")
        ctx_done = sem("ctx_done")
        ctx_ready = sem("ctx_ready")
        wo_done = sem("wo_done")
        x1_ready = sem("x1_ready")
        bn2_done = sem("bn2_done")
        stats2 = sem("stats2")
        var2_done = sem("var2_done")
        rstd2_done = sem("rstd2_done")
        xn2_ready = sem("xn2_ready")
        x2T_done = sem("x2T_done")
        x2T_ready = sem("x2T_ready")
        xg_hi_done = sem("xg_hi_done")
        xg_lo_done = sem("xg_lo_done")
        gate_done = sem("gate_done")
        gate_ready = sem("gate_ready")

        XPART = B // 4

        def batches(engine, batch):
            for b in range(-2, 4):
                batch(b, b % 2)
            with engine.Fori(2, (B - 2) // 2) as pair:
                for k in range(2):
                    batch(pair * 2 + k, k)
            for b in range(B - 2, B + 3):
                batch(b, b % 2)

        block = ctx.enter_context(nc.Block())

        @block.sync
        def _(sp):
            sp.dma_start(x_all[:, 0:XPART * TB, :], x_tiles[:, 0:XPART * TB, :]).then_inc(x_loaded[0], 16)
            sp.dma_start(wqk_raw[:, 0, :], w_q).then_inc(wqk_loaded, 16)
            sp.dma_start(wqk_raw[:, 1, :], w_k).then_inc(wqk_loaded, 16)
            sp.dma_start(wv_raw[:, :], w_v).then_inc(wv_loaded, 16)
            sp.dma_start(wo_sb[:, :, :], w_o.rearrange("(c p) n -> p c n", p=P)).then_inc(wo_loaded, 16)
            sp.dma_start(gate_sb[:, :], gate_w).then_inc(wo_loaded, 16)
            for i in range(1, 4):
                part = slice(i * XPART * TB, (i + 1) * XPART * TB)
                sp.dma_start(x_all[:, part, :], x_tiles[:, part, :]).then_inc(x_loaded[i], 16)
            sp.dma_start(w1_raw[:, :, :], w1.rearrange("e c h -> c e h")).then_inc(experts_loaded, 16)
            sp.dma_start(w2_sb[:, :, :, :], w2.rearrange("e (k p) c -> p e k c", p=P)).then_inc(experts_loaded, 16)

        @block.gpsimd
        def _(pool):
            nc.gpsimd.memset(ident[:, :], 0.0).then_inc(consts, 1)
            nc.gpsimd.memset(ident_bf[:, :], 0.0).then_inc(consts, 1)
            nc.gpsimd.memset(causal[:, :], 0.0).then_inc(consts, 1)
            nc.gpsimd.memset(neg_half[:, :], -0.5)
            nc.gpsimd.memset(eps_sb[:, :], EPS).then_inc(consts, 1)
            pool.wait_ge(consts, 4)
            for m in (ident, ident_bf):
                nc.gpsimd.affine_select(out=m[:, :], in_=m[:, :], compare_op=ALU.not_equal, fill=1.0, base=0,
                                        pattern=[[-1, P]], channel_multiplier=1).then_inc(consts2, 1)
            nc.gpsimd.affine_select(out=causal[:, :], in_=causal[:, :], compare_op=ALU.is_ge, fill=MASKED,
                                    base=0, pattern=[[-1, P]], channel_multiplier=1).then_inc(consts2, 1)

            pool.wait_ge(lows_ready, 2)

            def batch(b, par):
                for j in range(G):
                    u, r = b * G + j, j % RING
                    if has(u, UNITS):
                        pool.wait_ge(inv0, u + 1)
                        await_count(pool, t_done, (u - 1) * 3)
                        nc.gpsimd.tensor_tensor(
                            probn[r][:, 0:HG * P].rearrange("p (i k) -> p i k", i=HG),
                            prob[r][:, 0:HG * P].rearrange("p (i k) -> p i k", i=HG),
                            bcast(inv[:, r, 0, :], 2, P), ALU.mult).then_inc(normed, 1)
                    if has(u + 2, UNITS):
                        pool.wait_ge(qk_ready, u + 3)
                        await_count(pool, s1_done, u + 1)
                        nc.gpsimd.tensor_tensor(k_diag[r][:, :, :], bcast(f32(kT[r][:, :]), 1, HG),
                                                bcast(own_block[:, :], 2, T), ALU.mult).then_inc(k_ready, 1)
                    if j == 3 and has(b + 2, B):
                        pool.wait_ge(stats1, b + 3)
                        nc.gpsimd.tensor_tensor(var1[:, :], mv1[:, :, 1], eps_sb[:, :], ALU.add).then_inc(var1_done, 1)
                        pool.wait_ge(var1_done, b + 3)
                        nc.gpsimd.tensor_tensor(rstd1[:, :], var1[:, :], neg_half[:, :], ALU.pow).then_inc(rstd1_done, 1)
                    if j == 0 and has(b - 2, B):
                        pool.wait_ge(stats2, b - 1)
                        nc.gpsimd.tensor_tensor(var2[:, :], mv2[:, :, 1], eps_sb[:, :], ALU.add).then_inc(var2_done, 1)
                        pool.wait_ge(var2_done, b - 1)
                        nc.gpsimd.tensor_tensor(rstd2[:, :], var2[:, :], neg_half[:, :], ALU.pow).then_inc(rstd2_done, 1)
                    if has(u, UNITS):
                        pool.wait_ge(inv1, u + 1)
                        nc.gpsimd.tensor_tensor(
                            probn[r][:, HG * P:].rearrange("p (i k) -> p i k", i=HG),
                            prob[r][:, HG * P:].rearrange("p (i k) -> p i k", i=HG),
                            bcast(inv[:, r, 1, :], 2, T), ALU.mult).then_inc(normed, 1)

            batches(pool, batch)

        @block.scalar
        def _(act):
            act.wait_ge(wqk_loaded, 32)
            for w in range(2):
                nc.scalar.activation(wqk_hi[:, w, :, :, :],
                                     bcast(wqk_raw[:, w, :].rearrange("p (h d) -> p h d", h=H), 2, 4),
                                     ACT.Copy, scale=(DK ** -0.5 if w == 0 else 1.0)).then_inc(w_hi, 1)
            act.wait_ge(wv_loaded, 16)
            nc.scalar.activation(wv_hi[:, :], wv_raw[:, :], ACT.Copy).then_inc(w_hi, 1)

            def exps(r, block_, scores, keys, first, done):
                for i in range(HG):
                    last = nc.scalar.activation(
                        prob[r][:, first + i * keys:first + (i + 1) * keys], scores[:, i, :], ACT.Exp,
                        bias=neg_max[:, r, block_, i:i + 1], accum_out=sums[:, r, block_, i:i + 1])
                last.then_inc(done, 1)

            def batch(b, par):
                for j in range(G):
                    u = b * G + j
                    r1, r2, rm = (j + 1) % RING, j % RING, (j + 1) % RING
                    if has(u + 2, UNITS):
                        act.wait_ge(qk_done, u + 3)
                        await_count(act, qk_ready, u + 1)
                        nc.scalar.activation(qk_hi[r2][:, :, :],
                                             misc_ps[(3 * j) % 2][:, :].rearrange("p (a t) -> p a t", a=2),
                                             ACT.Copy).then_inc(qk_hi_done, 1)
                    if has(u + 1, UNITS):
                        act.wait_ge(max0, u + 2)
                        await_count(act, normed, u * 2)
                        exps(r1, 0, s0_ps, P, 0, exp0)
                    if has(u - 1, UNITS):
                        act.wait_ge(t_done, (u - 1) * 3 + 1)
                        await_count(act, ctx_done, u - 2)
                        nc.scalar.activation(probT[rm][:, 0:512], t_ps[rm][:, :], ACT.Copy).then_inc(t_act, 1)
                    if j == 1 and has(b + 1, B):
                        act.wait_ge(xT_done, b + 2)
                        nc.scalar.activation(xT_hi[1 - par][:, :], misc_ps[(3 * j + 1) % 2][:, 0:T],
                                             ACT.Copy).then_inc(xT_hi_done, 1)
                    if has(u + 1, UNITS):
                        act.wait_ge(max1, u + 2)
                        exps(r1, 1, s1_ps, T, HG * P, exp1)
                    if has(u + 2, UNITS):
                        w, q = u + 2, (j + 2) % G
                        vb = par if j < 2 else 1 - par
                        act.wait_ge(v_done, w + 1)
                        await_count(act, ctx_done, w - q - G)
                        nc.scalar.activation(v_sb[vb][:, q % 2, (q // 2) * 512:(q // 2 + 1) * 512],
                                             misc_ps[(3 * j) % 2][:, :], ACT.Copy).then_inc(v_ready, 1)
                    if has(u - 1, UNITS):
                        act.wait_ge(t_done, (u - 1) * 3 + 2)
                        nc.scalar.activation(probT[rm][:, 512:1024], t_ps[1 - rm][:, :], ACT.Copy).then_inc(t_act, 1)
                    if j == 2 and has(b - 2, B):
                        act.wait_ge(xn2_ready, b - 1)
                        nc.scalar.activation(xg_hi[:, bass.ds((b - 2) * TB, TB), :], xn2[:, :, :],
                                             ACT.Copy).then_inc(xg_hi_done, 1)

            batches(act, batch)

        @block.vector
        def _(dve):
            nc.vector.memset(low_row[:, :, :, :, :], 0.0).then_inc(low_rows, 1)
            dve.wait_ge(low_rows, 1)
            nc.vector.memset(low_row[:, 0, :, 2:4, :], -1.0)
            nc.vector.memset(low_row[:, 1, :, 1, :], -1.0)
            nc.vector.memset(low_row[:, 1, :, 3, :], -1.0).then_inc(low_rows, 1)
            dve.wait_ge(low_rows, 2)
            dve.wait_ge(consts2, 3)
            nc.vector.tensor_tensor(low_diag[:, :, :], low_row[:, :, :, :, :].rearrange("p a i r d -> p a (i r d)"),
                                    bcast(ident[:, :], 1, 2), ALU.mult).then_inc(low_diags, 1)
            dve.wait_ge(low_diags, 1)
            nc.vector.tensor_reduce(out=minus_low[:, :], in_=low_diag[:, :, :], axis=AX.X,
                                    op=ALU.add).then_inc(lows_ready, 1)
            nc.vector.tensor_reduce(out=own_block[:, :], in_=ident[:, :].rearrange("p (i r) -> p i r", i=HG),
                                    axis=AX.X, op=ALU.add).then_inc(lows_ready, 1)
            dve.wait_ge(lows_ready, 1)
            dve.wait_ge(w_hi, 2)
            nc.vector.scalar_tensor_tensor(
                out=wqk_lo[:, 0, :, 0, :],
                in0=wqk_raw[:, 0, :].rearrange("p (h d) -> p h d", h=H), scalar=DK ** -0.5,
                in1=f32(wqk_hi[:, 0, :, 0, :]), op0=ALU.mult, op1=ALU.subtract).then_inc(w_lo, 1)
            nc.vector.tensor_tensor(wqk_lo[:, 1, :, 0, :], wqk_raw[:, 1, :].rearrange("p (h d) -> p h d", h=H),
                                    f32(wqk_hi[:, 1, :, 0, :]), ALU.subtract).then_inc(w_lo, 1)
            dve.wait_ge(w_lo, 2)
            for w in range(2):
                nc.vector.tensor_copy(wqk_lo[:, w, :, 1:4, :], bcast(f32(wqk_lo[:, w, :, 0, :]), 2, 3)).then_inc(w_lo, 1)
            dve.wait_ge(w_hi, 3)
            nc.vector.tensor_tensor(wv_lo[:, :], wv_raw[:, :], f32(wv_hi[:, :]), ALU.subtract).then_inc(w_lo, 1)

            def norm_stats(src, bn, mv, bn_done, bn_count, stats_done):
                nc.vector.memset(holds_wait[:, :], 0.0)
                for tb in range(TB):
                    last = nc.vector.bn_stats(bn[:, tb, :], src(tb))
                last.then_inc(bn_done, 1)
                dve.wait_ge(bn_done, bn_count)
                nc.vector.memset(holds_wait[:, :], 0.0)
                for tb in range(TB):
                    last = nc.vector.bn_aggr(mv[:, tb, :], bn[:, tb, :])
                last.then_inc(stats_done, 1)

            def norm(dst, src, mv, rstd, done):
                for tb in range(TB):
                    last = nc.vector.tensor_scalar(dst[:, tb, :], src(tb), mv[:, tb, 0:1], rstd[:, tb:tb + 1],
                                                   ALU.subtract, ALU.mult)
                last.then_inc(done, 1)

            def batch(b, par):
                for j in range(G):
                    u = b * G + j
                    r1, r2, rm = (j + 1) % RING, j % RING, (j + 1) % RING
                    if has(u + 2, UNITS):
                        w = u + 2
                        qk_ps = misc_ps[(3 * j) % 2][:, :].rearrange("p (a t) -> p a t", a=2)
                        dve.wait_ge(qk_hi_done, w + 1)
                        await_count(dve, s1_done, w - 1)
                        await_count(dve, k_ready, w - 1)
                        nc.vector.scalar_tensor_tensor(out=qT[r2][:, :], in0=f32(qk_hi[r2][:, 0, :]),
                                                       scalar=minus_low[:, 0:1], in1=qk_ps[:, 0, :],
                                                       op0=ALU.mult, op1=ALU.add)
                        nc.vector.scalar_tensor_tensor(out=kT[r2][:, :], in0=f32(qk_hi[r2][:, 1, :]),
                                                       scalar=minus_low[:, 1:2], in1=qk_ps[:, 1, :],
                                                       op0=ALU.mult, op1=ALU.add).then_inc(qk_ready, 1)
                    if has(u + 1, UNITS):
                        dve.wait_ge(s1_done, u + 2)
                        nc.vector.tensor_reduce(out=neg_max[:, r1, 1, :], in_=s1_ps[:, :, :], axis=AX.X,
                                                op=ALU.max, negate=True).then_inc(max1, 1)
                    extra = misc_ps[(3 * j + 1) % 2]
                    if j == 0 and has(b - 3, B):
                        dve.wait_ge(gate_done, b - 2)
                        nc.vector.tensor_copy(gate_logit[:, bass.ds((b - 3) * TB, TB), :],
                                              extra[:, 0:TB * E].rearrange("p (t e) -> p t e", t=TB)).then_inc(gate_ready, 1)
                    if j == 1 and has(b + 1, B):
                        dve.wait_ge(xT_hi_done, b + 2)
                        nc.vector.tensor_tensor(xT_lo[1 - par][:, :], extra[:, 0:T], f32(xT_hi[1 - par][:, :]),
                                                ALU.subtract).then_inc(xT_ready, 1)
                    if j == 2 and has(b - 2, B):
                        dve.wait_ge(x2T_done, b - 1)
                        await_count(dve, gate_done, b - 2)
                        nc.vector.tensor_copy(xn2T[:, :], extra[:, 0:T]).then_inc(x2T_ready, 1)
                    if j == 3 and has(b - 1, B):
                        tiles = bass.ds((b - 1) * TB, TB)
                        dve.wait_ge(wo_done, b)
                        nc.vector.tensor_tensor(x_all[:, tiles, :], extra[:, 0:T].rearrange("p (t d) -> p t d", t=TB),
                                                x_all[:, tiles, :], ALU.add).then_inc(x1_ready, 1)
                    if has(u + 1, UNITS):
                        dve.wait_ge(exp0, u + 2)
                        nc.vector.reciprocal(inv[:, r1, 0, :], sums[:, r1, 0, :]).then_inc(inv0, 1)
                    if has(u - 2, UNITS):
                        cb = par if j >= 2 else 1 - par
                        g = (j - 2) % G
                        dve.wait_ge(ctx_done, u - 1)
                        await_count(dve, wo_done, b - 1 if j >= 2 else b - 2)
                        nc.vector.tensor_copy(ctxT[cb][:, 2 * g:2 * g + 2, :], ctx_ps[:, :, :]).then_inc(ctx_ready, 1)
                    if j == 0 and has(b + 1, B):
                        dve.wait_ge(rstd1_done, b + 2)
                        await_count(dve, xT_done, b + 1)
                        norm(xn1, lambda tb: x_all[:, (b + 1) * TB + tb, :], mv1, rstd1, xn1_ready)
                    if j == 1 and has(b - 2, B):
                        dve.wait_ge(rstd2_done, b - 1)
                        await_count(dve, x2T_done, b - 2)
                        await_count(dve, xg_lo_done, b - 2)
                        norm(xn2, lambda tb: x_all[:, (b - 2) * TB + tb, :], mv2, rstd2, xn2_ready)
                    if has(u + 2, UNITS):
                        dve.wait_ge(s0_done, u + 3)
                        nc.vector.tensor_reduce(out=neg_max[:, r2, 0, :], in_=s0_ps[:, :, :], axis=AX.X,
                                                op=ALU.max, negate=True).then_inc(max0, 1)
                    if j == 2 and has(b - 2, B):
                        dve.wait_ge(xg_hi_done, b - 1)
                        tiles = bass.ds((b - 2) * TB, TB)
                        nc.vector.tensor_tensor(xg_lo[:, tiles, :], xn2[:, :, :], f32(xg_hi[:, tiles, :]),
                                                ALU.subtract).then_inc(xg_lo_done, 1)
                    if j == 2 and has(b + 2, B):
                        if isinstance(b, int) and b == -2:
                            dve.wait_ge(x_loaded[0], 16)
                        if isinstance(b, int) and b == 2:
                            for i in range(1, 4):
                                dve.wait_ge(x_loaded[i], 16)
                        norm_stats(lambda tb: x_all[:, (b + 2) * TB + tb, :], bn6, mv1, bn1_done, b + 3, stats1)
                    if j == 3 and has(b - 1, B):
                        dve.wait_ge(x1_ready, b)
                        await_count(dve, rstd2_done, b - 1)
                        norm_stats(lambda tb: x_all[:, (b - 1) * TB + tb, :], bn6b, mv2, bn2_done, b, stats2)
                    if has(u - 1, UNITS):
                        dve.wait_ge(t_done, (u - 1) * 3 + 3)
                        await_count(dve, ctx_done, u - 2)
                        nc.vector.tensor_copy(probT[rm][:, 1024:1536], t_ps[rm][:, :]).then_inc(t_dve, 1)
                    if has(u + 1, UNITS):
                        dve.wait_ge(exp1, u + 2)
                        nc.vector.reciprocal(inv[:, r1, 1, :], sums[:, r1, 1, :]).then_inc(inv1, 1)

            batches(dve, batch)

        @block.tensor
        def _(pe):
            pe.wait_ge(consts2, 3)
            pe.wait_ge(w_hi, 3)
            pe.wait_ge(w_lo, 5)
            pe.wait_ge(wo_loaded, 32)

            def split_product(out_, w_h, w_l, x_h, x_l):
                nc.tensor.matmul(out_, w_h, x_h, start=True, stop=False)
                nc.tensor.matmul(out_, w_h, x_l, start=False, stop=False)
                return nc.tensor.matmul(out_, w_l, x_h, start=False, stop=True)

            def wo_product(to, context, tb):
                chunks = H * DV // P
                for c in range(chunks):
                    last = nc.tensor.matmul(to[:, tb * D:(tb + 1) * D], context[:, c, tb * P:(tb + 1) * P],
                                            wo_sb[:, c, :], start=(c == 0), stop=(c == chunks - 1))
                return last

            def batch(b, par):
                for j in range(G):
                    u = b * G + j
                    r1, r2, rm = (j + 1) % RING, j % RING, (j + 1) % RING
                    if has(u + 1, UNITS):
                        pe.wait_ge(k_ready, u + 2)
                        await_count(pe, exp1, u + 1)
                        for i in (0, 2):
                            nc.tensor.matmul(s1_ps[:, i:i + 2, :], qT[r1][:, P:T], k_diag[r1][:, i:i + 2, :],
                                             start=True, stop=False)
                            last = nc.tensor.matmul(s1_ps[:, i:i + 2, P:T], ident_bf[:, :], bcast(causal[:, :], 1, 2),
                                                    start=False, stop=True)
                        last.then_inc(s1_done, 1)
                    if j == 3 and has(b - 1, B):
                        wo_product(misc_ps[(3 * j + 1) % 2], ctxT[1 - par], 1).then_inc(wo_done, 1)
                    if has(u - 1, UNITS):
                        w = u - 1
                        pe.wait_ge(normed, w * 2 + 2)
                        q0 = probn[rm][:, 0:HG * P].rearrange("p (i k) -> p i k", i=HG)
                        q1 = probn[rm][:, HG * P:].rearrange("p (i k) -> p i k", i=HG)
                        for f in range(2):
                            await_count(pe, *((t_act, w * 2) if f == 0 else (t_dve, w)))
                            t = t_ps[rm if f == 0 else 1 - rm][:, :].rearrange("p (i q) -> p i q", i=2)
                            for i in range(2):
                                nc.tensor.transpose(t[:, i, 0:P], q0[:, 2 * f + i, :], ident[:, :])
                                last = nc.tensor.transpose(t[:, i, P:T], q1[:, 2 * f + i, 0:P], ident[:, :])
                            last.then_inc(t_done, 1)
                    if has(u - 2, UNITS):
                        w, g = u - 2, (j - 2) % G
                        vb = par if j >= 2 else 1 - par
                        pe.wait_ge(t_act, w * 2 + 2)
                        pe.wait_ge(t_dve, w + 1)
                        pe.wait_ge(v_ready, w - g + 2 * (g // 2) + 2)
                        await_count(pe, ctx_ready, w)
                        pt = probT[r2]
                        for pair in range(2):
                            for kb in range(TB):
                                for half in range(2):
                                    i = 2 * pair + half
                                    h = g * HG + i
                                    rhs = (pt[:, i * T:(i + 1) * T] if kb == 0 else
                                           pt[:, HG * T + i * P:HG * T + (i + 1) * P])
                                    last = nc.tensor.matmul(ctx_ps[half * DV:(half + 1) * DV, pair, kb * P:T],
                                                            v_sb[vb][:, kb, h * DV:(h + 1) * DV], rhs,
                                                            start=(kb == 0), stop=(kb == 1))
                        last.then_inc(ctx_done, 1)
                    if has(u + 2, UNITS):
                        w, q = u + 2, (j + 2) % G
                        xb = par if j < 2 else 1 - par
                        pe.wait_ge(qk_ready, w + 1)
                        toks = slice((q % 2) * P, (q % 2 + 1) * P)
                        cols = slice((q // 2) * 512, (q // 2 + 1) * 512)
                        split_product(misc_ps[(3 * j) % 2][:, :], xT_hi[xb][:, toks], xT_lo[xb][:, toks],
                                      wv_hi[:, cols], wv_lo[:, cols]).then_inc(v_done, 1)
                    if has(u - 1, UNITS):
                        w = u - 1
                        pe.wait_ge(t_act, w * 2 + 1)
                        t = t_ps[rm][:, :].rearrange("p (i q) -> p i q", i=HG)
                        for i in range(HG):
                            last = nc.tensor.transpose(t[:, i, :], q1[:, i, P:T], ident[:, :])
                        last.then_inc(t_done, 1)
                    if has(u + 2, UNITS):
                        pe.wait_ge(k_ready, u + 3)
                        await_count(pe, exp0, u + 2)
                        nc.tensor.matmul(s0_ps[:, :, :], qT[r2][:, 0:P], k_diag[r2][:, :, 0:P], start=True, stop=False)
                        nc.tensor.matmul(s0_ps[:, :, :], ident_bf[:, :], bcast(causal[:, :], 1, HG),
                                         start=False, stop=True).then_inc(s0_done, 1)
                    if has(u + 3, UNITS):
                        w, g = u + 3, (j + 3) % G
                        xb = par if j < 1 else 1 - par
                        heads = slice(g * HG, (g + 1) * HG)
                        qk_ps = misc_ps[(3 * j + 1) % 2]
                        pe.wait_ge(xT_ready, b + 1 if j < 1 else b + 2)
                        await_count(pe, *[(gate_ready, b - 2), (xT_ready, b + 2 if has(b + 1, B) else B), (x2T_ready, b - 1),
                                          (x1_ready, b)][j])
                        for a in range(2):
                            last = split_product(qk_ps[:, a * T:(a + 1) * T],
                                                 wqk_hi[:, a, heads, :, :].rearrange("p h r d -> p (h r d)"),
                                                 wqk_lo[:, a, heads, :, :].rearrange("p h r d -> p (h r d)"),
                                                 xT_hi[xb][:, :], xT_lo[xb][:, :])
                        last.then_inc(qk_done, 1)
                    extra = misc_ps[(3 * j + 2) % 2]
                    if has(u + 2, UNITS):
                        pe.wait_ge(v_ready, u + 3)
                    if j == 0 and has(b + 1, B):
                        pe.wait_ge(xn1_ready, b + 2)
                        for tb in range(TB):
                            last = nc.tensor.transpose(extra[:, tb * P:(tb + 1) * P], xn1[:, tb, :], ident[:, :])
                        last.then_inc(xT_done, 1)
                    if j == 1 and has(b - 2, B):
                        pe.wait_ge(xn2_ready, b - 1)
                        await_count(pe, gate_ready, b - 2)
                        for tb in range(TB):
                            last = nc.tensor.transpose(extra[:, tb * P:(tb + 1) * P], xn2[:, tb, :], ident[:, :])
                        last.then_inc(x2T_done, 1)
                    if j == 2 and has(b - 1, B):
                        pe.wait_ge(ctx_ready, b * G)
                        await_count(pe, x2T_ready, b - 1)
                        wo_product(extra, ctxT[1 - par], 0)
                    if j == 3 and has(b - 2, B):
                        pe.wait_ge(x2T_ready, b - 1)
                        for tb in range(TB):
                            last = nc.tensor.matmul(extra[:, tb * E:(tb + 1) * E], xn2T[:, tb * P:(tb + 1) * P],
                                                    gate_sb[:, :], start=True, stop=True)
                        last.then_inc(gate_done, 1)

            batches(pe, batch)


def experts(nc, out_tiles, x_all, xg_hi, xg_lo, gate_logit, ident, w1_raw, w2_sb, experts_loaded):
    with ExitStack() as ctx:
        def sb(name, shape, dt=F32):
            return ctx.enter_context(nc.sbuf_tensor(name, shape, dt))

        def ps(name, shape):
            return ctx.enter_context(nc.psum_tensor(name, shape, F32))

        def sem(name):
            return ctx.enter_context(nc.semaphore(name))

        TILES = B * TB
        EP = E // 2
        QB = 4
        STEPS = range(-4, B + 6)

        w1_hi = sb("w1_hi", [P, E, FF], F32R)
        w1_lo = sb("w1_lo", [P, E, FF], F32R)
        neg_top = sb("neg_top", [P, TILES])
        shifted = sb("shifted", [P, TILES, E])
        weight = sb("weight", [P, TILES, E])
        total = sb("total", [P, TILES])
        inv_total = sb("inv_total", [P, TILES])
        probs = sb("probs", [P, TB, B, E])
        left = sb("left", [P, T])
        top8 = sb("top8", [P, CAP // 8, 8])
        taken = sb("taken", [P, T])
        zeros = sb("zeros", [P, T])
        running = sb("running", [P, T])
        slot_of = sb("slot_of", [P, T])
        slotT = sb("slotT", [P, TB, B, E])
        slot_no = sb("slot_no", [P, CAP])
        pick = [sb(f"pick{r}", [P, TB, E * CAP], F32R) for r in range(RING)]
        xin_hi = [sb(f"xin_hi{r}", [P, E, QB, CAP], F32R) for r in range(RING)]
        xin_lo = [sb(f"xin_lo{r}", [P, E, QB, CAP], F32R) for r in range(RING)]
        hT = [sb(f"hT{r}", [P, 2, HC, QB * CAP]) for r in range(RING)]
        y_sb = [sb(f"y_sb{r}", [P, QB, EP, D]) for r in range(RING)]
        put = [w1_raw[:, r * TB:(r + 1) * TB, :] for r in range(RING)]
        putT = [sb(f"putT{r}", [P, EP, T]) for r in range(RING)]

        pick_hi_ps = ps("pick_hi_ps", [P, E, CAP])
        pick_lo_ps = ps("pick_lo_ps", [P, E, CAP])
        h_ps = [ps(f"h_ps{r}", [P, 2, QB * CAP]) for r in range(RING)]
        y_ps = ps("y_ps", [P, QB, D])
        putT_ps = ps("putT_ps", [P, EP, T])
        out_ps = ps("out_ps", [P, TB, D])

        def picked_ps(b):
            if b < QB and b % 2:
                turned = putT_ps[:, :, :].rearrange("p (a e) (s t) -> p a (e s) t", a=2, s=T // CAP)
                return turned[:, 0, :, :], turned[:, 1, :, :]
            return pick_hi_ps[:, :, :], pick_lo_ps[:, :, :]

        def picked_before(b):
            return b - 1 if b < QB else b

        numbered = sem("numbered")
        route = sem("route")
        weight_done = sem("weight_done")
        probsT_done = sem("probsT_done")
        rounds = sem("rounds")
        slots_done = sem("slots_done")
        slotT_done = sem("slotT_done")
        slotT_ready = sem("slotT_ready")
        w1_hi_done = sem("w1_hi_done")
        w1_ready = sem("w1_ready")
        pick_ready = sem("pick_ready")
        pick_done = sem("pick_done")
        xin_hi_ready = sem("xin_hi_ready")
        xin_lo_ready = sem("xin_lo_ready")
        h_done = sem("h_done")
        h_ready = sem("h_ready")
        y_done = sem("y_done")
        y_ready = sem("y_ready")
        put_ready = sem("put_ready")
        putT_done = sem("putT_done")
        putT_ready = sem("putT_ready")
        out_done = sem("out_done")
        out_ready = sem("out_ready")
        stored = sem("stored")

        block = ctx.enter_context(nc.Block())

        @block.sync
        def _(sp):
            with sp.Fori(0, B) as b:
                sp.wait_ge(out_ready, b + 1)
                sp.dma_start(out_tiles[:, bass.ds(b * TB, TB), :], x_all[:, bass.ds(b * TB, TB), :]).then_inc(stored, 16)
            sp.wait_ge(stored, 16 * B)

        @block.gpsimd
        def _(pool):
            nc.gpsimd.iota(slot_no[:, :], pattern=[[1, CAP]], base=1, channel_multiplier=0,
                           allow_small_or_imprecise_dtypes=True).then_inc(numbered, 1)
            nc.gpsimd.memset(zeros[:, :], 0.0).then_inc(numbered, 1)
            pool.wait_ge(experts_loaded, 32)
            for ep in range(EP):
                pair = slice(2 * ep, 2 * ep + 2)
                pool.wait_ge(w1_hi_done, ep + 1)
                nc.gpsimd.tensor_tensor(w1_lo[:, pair, :], w1_raw[:, pair, :], f32(w1_hi[:, pair, :]),
                                        ALU.subtract).then_inc(w1_ready, 1)

        @block.scalar
        def _(act):
            act.wait_ge(route, 2)
            nc.scalar.activation(weight[:, :, :], shifted[:, :, :], ACT.Exp).then_inc(weight_done, 1)
            act.wait_ge(experts_loaded, 32)
            for ep in range(EP):
                pair = slice(2 * ep, 2 * ep + 2)
                nc.scalar.activation(w1_hi[:, pair, :], w1_raw[:, pair, :], ACT.Copy).then_inc(w1_hi_done, 1)
            for n in STEPS:
                b = n + 4
                if has(b, B):
                    act.wait_ge(pick_done, b + 1)
                    await_count(act, h_done, (b // QB - 1) * 16)
                    nc.scalar.activation(xin_hi[b // QB % RING][:, :, b % QB, :], picked_ps(b)[0],
                                         ACT.Copy).then_inc(xin_hi_ready, 1)
                if has(n, B):
                    await_count(act, y_done, n - 1)
                    for k in range(4):
                        act.wait_ge(h_done, 4 * n + k + 1)
                        nc.scalar.activation(hT[n % RING][:, k // 2, 2 * (k % 2):2 * (k % 2) + 2, :],
                                             h_ps[k % 2][:, :, :], ACT.Gelu).then_inc(h_ready, 1)
                b = n - 5
                if has(b, B):
                    act.wait_ge(putT_done, b + 1)
                    await_count(act, out_done, b - 1)
                    nc.scalar.activation(putT[b % RING][:, :, :], putT_ps[:, :, :], ACT.Copy).then_inc(putT_ready, 1)

        @block.vector
        def _(dve):
            nc.vector.tensor_reduce(out=neg_top[:, :], in_=gate_logit[:, :, :], axis=AX.X, op=ALU.max,
                                    negate=True).then_inc(route, 1)
            dve.wait_ge(route, 1)
            nc.vector.tensor_tensor(shifted[:, :, :], gate_logit[:, :, :], bcast(neg_top[:, :], 2, E),
                                    ALU.add).then_inc(route, 1)
            dve.wait_ge(weight_done, 1)
            nc.vector.tensor_reduce(out=total[:, :], in_=weight[:, :, :], axis=AX.X, op=ALU.add).then_inc(route, 1)
            dve.wait_ge(route, 3)
            nc.vector.reciprocal(inv_total[:, :], total[:, :]).then_inc(route, 1)
            dve.wait_ge(route, 4)
            for tb in range(TB):
                last = nc.vector.tensor_tensor(
                    probs[:, tb, :, :], weight[:, :, :].rearrange("p (b t) e -> p t b e", t=TB)[:, tb, :, :],
                    bcast(inv_total[:, :].rearrange("p (b t) -> p t b", t=TB)[:, tb, :], 2, E), ALU.mult)
            last.then_inc(route, 1)
            dve.wait_ge(probsT_done, 1)
            nc.vector.tensor_copy(left[:, :], h_ps[0][:, 0, :]).then_inc(rounds, 1)
            for k in range(CAP // 8):
                dve.wait_ge(rounds, 2 * k + 1)
                nc.vector.max(out=top8[:, k, :], in_=left[:, :]).then_inc(rounds, 1)
                dve.wait_ge(rounds, 2 * k + 2)
                nc.vector.match_replace(out=left[:, :], in_to_replace=top8[:, k, :], in_values=left[:, :],
                                        imm_value=-1.0).then_inc(rounds, 1)
            dve.wait_ge(rounds, 2 * (CAP // 8) + 1)
            nc.vector.tensor_scalar(taken[:, :], left[:, :], 0.0, None, ALU.is_lt).then_inc(slots_done, 1)
            dve.wait_ge(slots_done, 1)
            dve.wait_ge(numbered, 2)
            nc.vector.tensor_tensor_scan(running[:, :], taken[:, :], zeros[:, :], 0.0, ALU.add, ALU.add).then_inc(slots_done, 1)
            dve.wait_ge(slots_done, 2)
            nc.vector.tensor_tensor(slot_of[:, :], running[:, :], taken[:, :], ALU.mult).then_inc(slots_done, 1)
            dve.wait_ge(slotT_done, 1)
            nc.vector.tensor_copy(slotT[:, :, :, :].rearrange("p t b e -> p t (b e)"),
                                  h_ps[1][:, 0, :].rearrange("p (t n) -> p t n", t=TB)).then_inc(slotT_ready, 1)
            dve.wait_ge(slotT_ready, 1)

            def picks(b):
                if has(b, B):
                    await_count(dve, pick_done, b - 1)
                    for tb in range(TB):
                        last = nc.vector.tensor_tensor(
                            pick[b % RING][:, tb, :].rearrange("p (e s) -> p e s", e=E),
                            bcast(slot_no[:, :], 1, E), bcast(slotT[:, tb, b, :], 2, CAP), ALU.is_equal)
                    last.then_inc(pick_ready, 1)

            picks(0)
            for n in STEPS:
                picks(n + 5)
                b = n + 4
                if has(b, B):
                    dve.wait_ge(pick_done, b + 1)
                    await_count(dve, h_done, (b // QB - 1) * 16)
                    nc.vector.tensor_copy(xin_lo[b // QB % RING][:, :, b % QB, :], picked_ps(b)[1]).then_inc(xin_lo_ready, 1)
                m = n - 1
                if has(m, B):
                    dve.wait_ge(y_done, m + 1)
                    await_count(dve, out_done, (m // QB - 1) * QB)
                    nc.vector.tensor_copy(y_sb[m // QB % RING][:, :, m % EP, :], y_ps[:, :, :]).then_inc(y_ready, 1)
                b = n - 4
                if has(b, B):
                    if b == 0:
                        dve.wait_ge(w1_ready, EP)
                        dve.wait_ge(w1_hi_done, EP)
                    await_count(dve, putT_done, b - 1)
                    for tb in range(TB):
                        for e in range(E):
                            last = nc.vector.tensor_scalar(
                                put[b % RING][:, tb, e * CAP:(e + 1) * CAP], slot_no[:, :],
                                slotT[:, tb, b, e:e + 1], probs[:, tb, b, e:e + 1], ALU.is_equal, ALU.mult)
                    last.then_inc(put_ready, 1)
                b = n - 6
                if has(b, B):
                    dve.wait_ge(out_done, b + 1)
                    nc.vector.tensor_tensor(x_all[:, b * TB:(b + 1) * TB, :], out_ps[:, :, :],
                                            x_all[:, b * TB:(b + 1) * TB, :], ALU.add).then_inc(out_ready, 1)

        @block.tensor
        def _(pe):
            pe.wait_ge(route, 5)
            for tb in range(TB):
                last = nc.tensor.transpose(h_ps[0][:, 0, tb * P:(tb + 1) * P], probs[:, tb, :, :].rearrange("p b e -> p (b e)"), ident[:, :])
            last.then_inc(probsT_done, 1)
            pe.wait_ge(slots_done, 3)
            for tb in range(TB):
                last = nc.tensor.transpose(h_ps[1][:, 0, tb * P:(tb + 1) * P], slot_of[:, tb * P:(tb + 1) * P], ident[:, :])
            last.then_inc(slotT_done, 1)
            pe.wait_ge(slotT_ready, 1)
            for n in STEPS:
                b = n + 4
                if has(b, B):
                    pe.wait_ge(pick_ready, b + 1)
                    await_count(pe, xin_hi_ready, picked_before(b))
                    await_count(pe, xin_lo_ready, picked_before(b))
                    for part, to in zip((xg_hi, xg_lo), picked_ps(b)):
                        for tb in range(TB):
                            last = nc.tensor.matmul(to, part[:, b * TB + tb, :], pick[b % RING][:, tb, :],
                                                    start=(tb == 0), stop=(tb == TB - 1))
                    last.then_inc(pick_done, 1)
                if has(n, B):
                    if n < EP:
                        pe.wait_ge(w1_ready, n + 1)
                    quarter = n // QB
                    pe.wait_ge(xin_hi_ready, (quarter + 1) * QB)
                    pe.wait_ge(xin_lo_ready, (quarter + 1) * QB)
                    for k in range(4):
                        e = 2 * (n % EP) + k // 2
                        await_count(pe, h_ready, 4 * n + k - 1)
                        for c in range(2):
                            hidden = slice((2 * (k % 2) + c) * P, (2 * (k % 2) + c + 1) * P)
                            xh = xin_hi[quarter % RING][:, e, :, :].rearrange("p b s -> p (b s)")
                            xl = xin_lo[quarter % RING][:, e, :, :].rearrange("p b s -> p (b s)")
                            to = h_ps[k % 2][:, c, :]
                            nc.tensor.matmul(to, w1_hi[:, e, hidden], xh, start=True, stop=False)
                            nc.tensor.matmul(to, w1_hi[:, e, hidden], xl, start=False, stop=False)
                            last = nc.tensor.matmul(to, w1_lo[:, e, hidden], xh, start=False, stop=True)
                        last.then_inc(h_done, 1)
                m = n - 1
                if has(m, B):
                    pe.wait_ge(h_ready, 4 * (m + 1))
                    await_count(pe, y_ready, m)
                    for q in range(QB):
                        for c in range(HC):
                            for half in range(2):
                                last = nc.tensor.matmul(y_ps[half * CAP:(half + 1) * CAP, q, :],
                                                        hT[m % RING][:, half, c, q * CAP:(q + 1) * CAP],
                                                        w2_sb[:, 2 * (m % EP) + half, c, :],
                                                        start=(c == 0), stop=(c == HC - 1))
                    last.then_inc(y_done, 1)
                b = n - 5
                if has(b, B):
                    pe.wait_ge(put_ready, b + 1)
                    await_count(pe, putT_ready, b)
                    for ep in range(EP):
                        for tb in range(TB):
                            last = nc.tensor.transpose(putT_ps[:, ep, tb * P:(tb + 1) * P],
                                                       put[b % RING][:, tb, ep * P:(ep + 1) * P], ident[:, :])
                    last.then_inc(putT_done, 1)
                b = n - 6
                if has(b, B):
                    pe.wait_ge(putT_ready, b + 1)
                    pe.wait_ge(y_ready, (b // QB + 1) * EP)
                    await_count(pe, out_ready, b)
                    for tb in range(TB):
                        for ep in range(EP):
                            last = nc.tensor.matmul(out_ps[:, tb, :], putT[b % RING][:, ep, tb * P:(tb + 1) * P],
                                                    y_sb[b // QB % RING][:, b % QB, ep, :],
                                                    start=(ep == 0), stop=(ep == EP - 1))
                    last.then_inc(out_done, 1)


INPUTS = ["L0_attn_x", "L0_attn_Wq", "L0_attn_Wk", "L0_attn_Wv", "L0_attn_Wo",
          "L0_ffn_gate_w", "L0_ffn_w1", "L0_ffn_w2"]


def kernel(**inputs):
    import concourse.bacc as bacc
    from concourse.bass_utils import run_bass_kernel_spmd

    nc = bacc.Bacc("TRN2", target_bir_lowering=False, num_devices=1)
    arrays, aps = {}, []
    for name in INPUTS:
        a = np.ascontiguousarray(inputs[name])
        arrays[f"in_{name}"] = a
        aps.append(nc.dram_tensor(f"in_{name}", a.shape, mybir.dt.from_np(a.dtype), kind="ExternalInput").ap())
    result = nc.dram_tensor("out_0", [B, T, D], F32, kind="ExternalOutput").ap()
    block_kernel(nc, *aps, result)
    r = run_bass_kernel_spmd(nc, [arrays], core_ids=[0])
    return r.results[0]["out_0"]
```
